# Optimizing a Trainium2 kernel written in Bass

```python
import numpy as np
import jax
import jax.numpy as jnp

def _softmax(x, axis=-1):
    return jax.nn.softmax(x, axis=axis)

def _gelu(x):
    return jax.nn.gelu(x, approximate=True)

def _silu(x):
    return jax.nn.silu(x)

def _sigmoid(x):
    return jax.nn.sigmoid(x)

def _layernorm(x, axis=-1, eps=1e-05):
    m = jnp.mean(x, axis=axis, keepdims=True)
    v = jnp.var(x, axis=axis, keepdims=True)
    return (x - m) / jnp.sqrt(v + eps)

def _scatter_add(tgt, idx, src, axis=0):
    return tgt.at[idx].add(src)

def _segment_sum(src, seg, n):
    return jax.ops.segment_sum(src, seg, n)
kernel_name = 'mk_gnn_resnorm_d4_gnn_r8_f93c7e'

def setup_inputs(seed: int=0):
    np.random.seed(seed)
    _w = jnp.asarray

    def _rec_inputs():
        import jax
        import jax.numpy as jnp
        _gk = jax.random.key(seed)
        x = -0.000202 + 1 * jax.random.normal(jax.random.fold_in(_gk, 1), (6250, 128), jnp.float32)
        _s = jax.random.randint(jax.random.fold_in(_gk, 2), (50000,), 0, 6250, jnp.int32)
        _d = jax.random.randint(jax.random.fold_in(_gk, 3), (50000,), 0, 6250, jnp.int32)
        _loop = jnp.arange(6250, dtype=jnp.int32)
        src = jnp.concatenate([_s, _d, _loop])
        dst = jnp.concatenate([_d, _s, _loop])
        _o = jnp.argsort(dst, stable=True)
        src = src[_o]
        dst = dst[_o]
        edge_type_40 = jax.random.randint(jax.random.fold_in(_gk, 14), (106250,), 0, 40, jnp.int32)
        return (x, src, dst, edge_type_40)
    x, src, dst, edge_type_40 = _rec_inputs()

    def _L0_gnn_setup():
        import jax, jax.numpy as jnp
        import numpy as np
        N, E, D, R = (6250, 200000, 128, 40)
        DIFFUSION_STEPS = 1
        key = jax.random.key(seed)
        ks = jax.random.split(key, 8)
        return {'h': jax.random.normal(ks[0], (N, D), dtype=jnp.float32), 'rFeatures': jax.random.normal(ks[1], (R, D), dtype=jnp.float32), 'relation_weights': jax.random.normal(ks[2], (R, D, D), dtype=jnp.float32) * (1.0 / np.sqrt(D)), 'loop_weight': jax.random.normal(ks[3], (D, D), dtype=jnp.float32) * (1.0 / np.sqrt(D)), 'norm': jax.random.uniform(ks[4], (N, 1), dtype=jnp.float32), 'edge_src': jax.random.randint(ks[5], (E,), 0, N, dtype=jnp.int32), 'edge_dst': jax.random.randint(ks[6], (E,), 0, N, dtype=jnp.int32), 'edge_type': jax.random.randint(ks[7], (E,), 0, R, dtype=jnp.int32)}
    _L0_gnn_all = _L0_gnn_setup()
    _L0_gnn_in = {k: v for k, v in _L0_gnn_all.items() if k in ('rFeatures', 'relation_weights', 'loop_weight')}
    del _L0_gnn_all

    def _L1_gnn_setup():
        import jax, jax.numpy as jnp
        import numpy as np
        N, E = (6250, 100000)
        IN_DIM, HID, HEADS, OUT_DIM = (128, 64, 4, 128)
        NEG_SLOPE = 0.2

        def _gat_forward(x, edge_index, W, att_src, att_dst, bias, fc_w, fc_b):
            n = x.shape[0]
            h = (x @ W).reshape(n, HEADS, HID)
            loops = jnp.arange(n, dtype=edge_index.dtype)
            src = jnp.concatenate([edge_index[0], loops])
            dst = jnp.concatenate([edge_index[1], loops])
            a_src = jnp.einsum('nhf,hf->nh', h, att_src)
            a_dst = jnp.einsum('nhf,hf->nh', h, att_dst)
            e = jax.nn.leaky_relu(a_src[src] + a_dst[dst], NEG_SLOPE)
            m = jax.ops.segment_max(e, dst, num_segments=n)
            ex = jnp.exp(e - m[dst])
            denom = jax.ops.segment_sum(ex, dst, num_segments=n)
            alpha = ex / denom[dst]
            msg = h[src] * alpha[:, :, None]
            agg = jax.ops.segment_sum(msg, dst, num_segments=n)
            out = agg.reshape(n, HEADS * HID) + bias
            out = jax.nn.relu(out)
            return out @ fc_w + fc_b
        key = jax.random.key(seed)
        ks = jax.random.split(key, 8)
        s = 1.0 / np.sqrt(IN_DIM)
        x = jax.random.normal(ks[0], (N, IN_DIM), dtype=jnp.float32)
        edge_index = jax.random.randint(ks[1], (2, E), 0, N, dtype=jnp.int64)
        W = jax.random.uniform(ks[2], (IN_DIM, HEADS * HID), jnp.float32, -s, s)
        att_src = jax.random.uniform(ks[3], (HEADS, HID), jnp.float32, -s, s)
        att_dst = jax.random.uniform(ks[4], (HEADS, HID), jnp.float32, -s, s)
        bias = jnp.zeros((HEADS * HID,), jnp.float32)
        sf = 1.0 / np.sqrt(HEADS * HID)
        fc_w = jax.random.uniform(ks[5], (HEADS * HID, OUT_DIM), jnp.float32, -sf, sf)
        fc_b = jax.random.uniform(ks[6], (OUT_DIM,), jnp.float32, -sf, sf)
        return {'x': x, 'edge_index': edge_index, 'W': W, 'att_src': att_src, 'att_dst': att_dst, 'bias': bias, 'fc_w': fc_w, 'fc_b': fc_b}
    _L1_gnn_all = _L1_gnn_setup()
    _L1_gnn_in = {k: v for k, v in _L1_gnn_all.items() if k in ('W', 'att_src', 'att_dst', 'bias', 'fc_w', 'fc_b')}
    del _L1_gnn_all

    def _L2_gnn_setup():
        import jax, jax.numpy as jnp
        import numpy as np
        N_NODES = 6250
        N_EDGES = 100000
        F_IN = 128
        N_HEADS = 4
        F_OUT = 32
        key = jax.random.key(seed)
        ks = jax.random.split(key, 6)
        x = jax.random.normal(ks[0], (N_NODES, F_IN), dtype=jnp.float32)
        edge_index = jax.random.randint(ks[1], (2, N_EDGES), 0, N_NODES, dtype=jnp.int64)
        lim = float(np.sqrt(6.0 / (F_IN + N_HEADS * F_OUT)))
        W_proj = jax.random.uniform(ks[2], (F_IN, N_HEADS * F_OUT), jnp.float32, -lim, lim)
        W_skip = jax.random.uniform(ks[3], (F_IN, N_HEADS * F_OUT), jnp.float32, -lim, lim)
        score_src = jax.random.normal(ks[4], (1, N_HEADS, F_OUT), dtype=jnp.float32) * 0.1
        score_tgt = jax.random.normal(ks[5], (1, N_HEADS, F_OUT), dtype=jnp.float32) * 0.1
        bias = jnp.zeros((N_HEADS * F_OUT,), dtype=jnp.float32)
        return {'x': x, 'edge_index': edge_index, 'W_proj': W_proj, 'score_src': score_src, 'score_tgt': score_tgt, 'W_skip': W_skip, 'bias': bias}
    _L2_gnn_all = _L2_gnn_setup()
    _L2_gnn_in = {k: v for k, v in _L2_gnn_all.items() if k in ('W_proj', 'score_src', 'score_tgt', 'W_skip', 'bias')}
    del _L2_gnn_all

    def _L3_gnn_setup():
        import jax, jax.numpy as jnp
        import numpy as np
        K = 8
        NITER = 6
        TAU = 1.0
        EPS = 1e-12
        N_NODES = 6250
        D = 128
        N_EDGES = 62500

        def _factor_normalize(v):
            nrm = jnp.linalg.norm(v, axis=-1, keepdims=True)
            return v / jnp.maximum(nrm, EPS)
        key = jax.random.key(seed)
        kx, ke = jax.random.split(key)
        x = jax.random.normal(kx, (N_NODES, D), dtype=jnp.float32)
        edge_index = jax.random.randint(ke, (2, N_EDGES), 0, N_NODES, dtype=jnp.int64)
        return {'x': x, 'edge_index': edge_index}
    _L3_gnn_all = _L3_gnn_setup()
    _L3_gnn_in = {k: v for k, v in _L3_gnn_all.items() if k in ()}
    del _L3_gnn_all
    return {'x': x, 'src': src, 'dst': dst, 'edge_type_40': edge_type_40, 'L0_gnn_rFeatures': _L0_gnn_in['rFeatures'], 'L0_gnn_relation_weights': _L0_gnn_in['relation_weights'], 'L0_gnn_loop_weight': _L0_gnn_in['loop_weight'], 'L1_gnn_W': _L1_gnn_in['W'], 'L1_gnn_att_src': _L1_gnn_in['att_src'], 'L1_gnn_att_dst': _L1_gnn_in['att_dst'], 'L1_gnn_bias': _L1_gnn_in['bias'], 'L1_gnn_fc_w': _L1_gnn_in['fc_w'], 'L1_gnn_fc_b': _L1_gnn_in['fc_b'], 'L2_gnn_W_proj': _L2_gnn_in['W_proj'], 'L2_gnn_score_src': _L2_gnn_in['score_src'], 'L2_gnn_score_tgt': _L2_gnn_in['score_tgt'], 'L2_gnn_W_skip': _L2_gnn_in['W_skip'], 'L2_gnn_bias': _L2_gnn_in['bias']}

def reference(x, src, dst, edge_type_40, L0_gnn_rFeatures, L0_gnn_relation_weights, L0_gnn_loop_weight, L1_gnn_W, L1_gnn_att_src, L1_gnn_att_dst, L1_gnn_bias, L1_gnn_fc_w, L1_gnn_fc_b, L2_gnn_W_proj, L2_gnn_score_src, L2_gnn_score_tgt, L2_gnn_W_skip, L2_gnn_bias):
    import jax
    import jax.numpy as jnp

    def _L0_gnn_ref(h, rFeatures, relation_weights, loop_weight, norm, edge_src, edge_dst, edge_type):
        import jax, jax.numpy as jnp
        import numpy as np
        N, E, D, R = (6250, 200000, 128, 40)
        DIFFUSION_STEPS = 1
        n, d = h.shape
        r = relation_weights.shape[0]
        seg = edge_dst.astype(jnp.int32) * r + edge_type.astype(jnp.int32)
        for _ in range(DIFFUSION_STEPS):
            S = jax.ops.segment_sum(h[edge_src], seg, num_segments=n * r).reshape(n, r, d)
            cnt = jax.ops.segment_sum(jnp.ones(edge_src.shape, h.dtype), seg, num_segments=n * r).reshape(n, r)
            agg = jnp.einsum('nrd,rdf->nf', S, relation_weights) + cnt @ rFeatures
            h = agg * norm
        h = jax.nn.relu(h + h @ loop_weight)
        return h

    def _L1_gnn_ref(x, edge_index, W, att_src, att_dst, bias, fc_w, fc_b):
        import jax, jax.numpy as jnp
        import numpy as np
        N, E = (6250, 100000)
        IN_DIM, HID, HEADS, OUT_DIM = (128, 64, 4, 128)
        NEG_SLOPE = 0.2

        def _gat_forward(x, edge_index, W, att_src, att_dst, bias, fc_w, fc_b):
            n = x.shape[0]
            h = (x @ W).reshape(n, HEADS, HID)
            loops = jnp.arange(n, dtype=edge_index.dtype)
            src = jnp.concatenate([edge_index[0], loops])
            dst = jnp.concatenate([edge_index[1], loops])
            a_src = jnp.einsum('nhf,hf->nh', h, att_src)
            a_dst = jnp.einsum('nhf,hf->nh', h, att_dst)
            e = jax.nn.leaky_relu(a_src[src] + a_dst[dst], NEG_SLOPE)
            m = jax.ops.segment_max(e, dst, num_segments=n)
            ex = jnp.exp(e - m[dst])
            denom = jax.ops.segment_sum(ex, dst, num_segments=n)
            alpha = ex / denom[dst]
            msg = h[src] * alpha[:, :, None]
            agg = jax.ops.segment_sum(msg, dst, num_segments=n)
            out = agg.reshape(n, HEADS * HID) + bias
            out = jax.nn.relu(out)
            return out @ fc_w + fc_b
        return _gat_forward(x, edge_index, W, att_src, att_dst, bias, fc_w, fc_b)

    def _L2_gnn_ref(x, edge_index, W_proj, score_src, score_tgt, W_skip, bias):
        import jax, jax.numpy as jnp
        import numpy as np
        N_NODES = 6250
        N_EDGES = 100000
        F_IN = 128
        N_HEADS = 4
        F_OUT = 32
        N = x.shape[0]
        H, F = (score_src.shape[1], score_src.shape[2])
        src, tgt = (edge_index[0], edge_index[1])
        proj = (x @ W_proj).reshape(N, H, F)
        s_src = jnp.sum(proj * score_src, axis=-1)
        s_tgt = jnp.sum(proj * score_tgt, axis=-1)
        scores = jax.nn.leaky_relu(s_src[src] + s_tgt[tgt], negative_slope=0.2)
        exp_scores = jnp.exp(scores - jnp.max(scores))
        denom = jax.ops.segment_sum(exp_scores, tgt, num_segments=N)
        att = exp_scores / (denom[tgt] + 1e-16)
        weighted = proj[src] * att[:, :, None]
        out = jax.ops.segment_sum(weighted, tgt, num_segments=N)
        if out.shape[-1] == x.shape[-1]:
            out = out + x[:, None, :]
        else:
            out = out + (x @ W_skip).reshape(N, H, F)
        out = out.reshape(N, H * F) + bias
        return jax.nn.elu(out)

    def _L3_gnn_ref(x, edge_index):
        import jax, jax.numpy as jnp
        import numpy as np
        K = 8
        NITER = 6
        TAU = 1.0
        EPS = 1e-12
        N_NODES = 6250
        D = 128
        N_EDGES = 62500

        def _factor_normalize(v):
            nrm = jnp.linalg.norm(v, axis=-1, keepdims=True)
            return v / jnp.maximum(nrm, EPS)
        n, d = x.shape
        k, dd = (K, d // K)
        src, trg = (edge_index[0], edge_index[1])
        xk = _factor_normalize(x.reshape(n, k, dd))
        z = xk[src]
        u = xk
        for _ in range(NITER):
            p = jax.nn.softmax(jnp.sum(z * u[trg], axis=2) / TAU, axis=1)
            msg = (z * p[:, :, None]).reshape(-1, d)
            agg = jax.ops.segment_sum(msg, trg, num_segments=n)
            u = _factor_normalize(agg.reshape(n, k, dd) + xk)
        return u.reshape(n, d)
    edge_index = jnp.stack([src, dst])
    deg = jnp.maximum(jax.ops.segment_sum(jnp.ones(dst.shape, jnp.float32), dst, num_segments=6250), 1.0)
    deg_isqrt = deg ** (-0.5)
    x = _layernorm(x + _L0_gnn_ref(x, L0_gnn_rFeatures, L0_gnn_relation_weights, L0_gnn_loop_weight, deg_isqrt[:, None], src, dst, edge_type_40), axis=-1)
    x = _layernorm(x + _L1_gnn_ref(x, edge_index, L1_gnn_W, L1_gnn_att_src, L1_gnn_att_dst, L1_gnn_bias, L1_gnn_fc_w, L1_gnn_fc_b), axis=-1)
    x = _layernorm(x + _L2_gnn_ref(x, edge_index, L2_gnn_W_proj, L2_gnn_score_src, L2_gnn_score_tgt, L2_gnn_W_skip, L2_gnn_bias), axis=-1)
    x = _layernorm(x + _L3_gnn_ref(x, edge_index), axis=-1)
    return x

_drawn_inputs = setup_inputs


def setup_inputs(seed=0):
    import zlib

    import numpy as np

    out = dict(_drawn_inputs(seed))
    spreads = {'L1_gnn_bias': (0.0, 0.1), 'L2_gnn_bias': (0.0, 0.1)}
    factors = {'L1_gnn_att_src': 6.124, 'L1_gnn_att_dst': 8.0}
    for name, (base, spread) in spreads.items():
        noise = np.random.default_rng([zlib.crc32(name.encode()), seed]).standard_normal(out[name].shape)
        drawn = base * np.exp(spread * noise) if base else spread * noise
        out[name] = jnp.asarray(drawn.astype(out[name].dtype))
    for name, factor in factors.items():
        out[name] = (out[name] * factor).astype(out[name].dtype)
    return out
```

```python
import concourse.bass as bass
from concourse import mybir
from contextlib import ExitStack

fp32 = mybir.dt.float32
bf16 = mybir.dt.bfloat16
i32 = mybir.dt.int32
ALU = mybir.AluOpType
ACT = mybir.ActivationFunctionType
AX = mybir.AxisListType
DVE_ENGINE = [mybir.EngineType.DVE]
PE_ENGINE = [mybir.EngineType.PE]

P = 128
D = 128
N = 6250
E = 106250
R = 40
HEADS = 4
F1 = 64
F2 = 32
CAPS, CD = 8, 16
ROUTINGS = 6

NT = -(-N // P)
NTP = NT + 1
NP = NTP * P
LAST = N - (NT - 1) * P

EJ = -(-E // P)
ELAST = E - (P - 1) * EJ
SU = 16
EJP = -(-EJ // SU) * SU
RB = 10
EJR = -(-EJ // (2 * RB)) * 2 * RB

NCH = -(-(EJ + NT) // 16) * 16
CQ = 4
NQ = NCH // CQ
RING = 4
SLOTS = P * NCH
OUTSIDE = 1 << 20

BIG = 1e30


def sweep(eng, stages):
    def peeled(k):
        for off, fn in stages:
            if 0 <= k + off < NQ:
                fn(k + off, (k + off) % RING)

    first, last = 2, (NQ - 4) // RING
    for k in range(-4, first * RING):
        peeled(k)
    with eng.Fori(first, last) as i:
        for s in range(RING):
            for off, fn in stages:
                fn(i * RING + (s + off), (s + off) % RING)
    for k in range(last * RING, NQ + 4):
        peeled(k)


def gnn_resnorm_kernel(nc, x_in, src_in, dst_in, type_in, rfeat, relw, loopw,
                       w1, att_s, att_d, bias1, fcw, fcb,
                       wproj, sc_s, sc_t, wskip, bias2, out):
    ctx = ExitStack()
    with ctx:
        def sb(name, shape, dt, where=ctx):
            return where.enter_context(nc.sbuf_tensor(name, shape, dt))

        def sem(name, where=None):
            if where is None:
                return ctx.enter_context(nc.semaphore(name))
            where.sems.append(nc.alloc_semaphore(name))
            return where.sems[-1]

        class Phase(ExitStack):

            def __init__(self):
                super().__init__()
                self.sems = []

            def __exit__(self, *exc):
                if self.sems and exc[0] is None:
                    nc.clear_and_free_semaphores(self.sems)
                    nc.all_engine_barrier()
                return super().__exit__(*exc)

        s_tick = sem("gather_quads_begun")
        ps = ctx.enter_context(nc.psum_tensor("ps", [P, 8, 512], fp32))

        y_tab = nc.dram_tensor("y_tab", [NP * R, D], fp32, kind="Internal").ap()
        t1_tab = nc.dram_tensor("t1_tab", [NP, HEADS * F1 + HEADS], fp32, kind="Internal").ap()
        a1_tab = nc.dram_tensor("a1_tab", [NP, HEADS], fp32, kind="Internal").ap()
        t2_tab = nc.dram_tensor("t2_tab", [NP, HEADS * F2 + HEADS], fp32, kind="Internal").ap()
        a2_tab = nc.dram_tensor("a2_tab", [NP, HEADS], fp32, kind="Internal").ap()
        x3_tab = nc.dram_tensor("x3_tab", [NP, D], fp32, kind="Internal").ap()
        z_tab = nc.dram_tensor("z_tab", [NQ, P, CQ * D], fp32, kind="Internal").ap()
        rec_tab = nc.dram_tensor("rec_tab", [SLOTS, 4], i32, kind="Internal").ap()
        dl_tab = nc.dram_tensor("dl_tab", [NCH, P], bf16, kind="Internal").ap()

        x_sb = sb("x_sb", [P, NTP, D], fp32)
        ident = sb("ident", [P, P], fp32)
        lane = sb("lane", [P, P], fp32)
        part = sb("part", [P, 1], fp32)
        y_row = sb("y_row", [P, NCH], i32)
        src_row = sb("src_row", [P, NCH], i32)
        dl_f = sb("dl_f", [P, NCH], fp32)
        chunk_tile = sb("chunk_tile", [1, NCH], i32)

        with Phase() as ph:
            src_e = sb("src_e", [P, EJP], i32, ph)
            dst_e = sb("dst_e", [P, EJP], i32, ph)
            typ_e = sb("typ_e", [P, EJP], i32, ph)
            tile_f = sb("tile_f", [P, EJR], fp32, ph)
            rank = sb("rank", [P, EJR], fp32, ph)
            eid = sb("eid", [P, EJP], fp32, ph)
            tmp_f = sb("tmp_f", [P, EJR], fp32, ph)
            tmp_i = sb("tmp_i", [P, EJR], i32, ph)
            row_i = sb("row_i", [P, EJP], i32, ph)
            pay = sb("pay", [P, EJP, 4], i32, ph)
            blank = sb("blank", [P, NCH, 4], i32, ph)
            tri = sb("tri", [P, P], bf16, ph)
            ones = sb("ones", [P, P], bf16, ph)
            onesf = sb("onesf", [P, P], fp32, ph)
            hot = sb("hot", [P, 2, RB, NT], bf16, ph)
            placed = sb("placed", [P, 2, RB, NT], fp32, ph)
            run = sb("run", [P, NT], fp32, ph)
            nch_f = sb("nch_f", [P, NT], fp32, ph)
            nch_i = sb("nch_i", [P, NT], i32, ph)
            ends = sb("ends", [P, NT], fp32, ph)
            base = sb("base", [P, NT], fp32, ph)
            end_col = sb("end_col", [NT, 1], fp32, ph)
            chunk_no = sb("chunk_no", [NT, NCH], fp32, ph)
            past = sb("past", [NT, NCH], fp32, ph)

            s_in = sem("edges_in", ph)
            s_iota = sem("iotas_made", ph)
            s_ms = sem("buffers_cleared", ph)
            s_const = sem("constants_made", ph)
            s_blank = sem("records_blanked", ph)
            s_hot = sem("hot_made", ph)
            s_pre = sem("prefixes_counted", ph)
            s_use = sem("prefixes_used", ph)
            s_v = sem("bucket_arithmetic", ph)
            s_ec = sem("ends_transposed", ph)
            s_past = sem("past_made", ph)
            s_tile = sem("chunk_tiles_summed", ph)

            with nc.Block() as block:
                @block.sync
                def _(sp):
                    sp.wait_ge(s_ms, 1)
                    for a, b in ((src_e, src_in), (dst_e, dst_in), (typ_e, type_in)):
                        sp.dma_start(a[0:P - 1, 0:EJ], b[0:(P - 1) * EJ].rearrange("(p j) -> p j", j=EJ))\
                          .then_inc(s_in, 16)
                        sp.dma_start(a[P - 1:P, 0:ELAST],
                                     b[(P - 1) * EJ:E].rearrange("(p j) -> p j", p=1)).then_inc(s_in, 16)
                    sp.dma_start(x_sb[:, 0:NT - 1, :],
                                 x_in[0:(NT - 1) * P, :].rearrange("(t p) d -> p t d", p=P)).then_inc(s_in, 16)
                    sp.dma_start(x_sb[0:LAST, NT - 1, :], x_in[(NT - 1) * P:N, :]).then_inc(s_in, 16)
                    sp.wait_ge(s_const, 2)
                    sp.dma_start(rec_tab.rearrange("(p c) w -> p c w", p=P), blank[:]).then_inc(s_blank, 16)
                    sp.wait_ge(s_in, 16 * 8)
                    sp.wait_ge(s_blank, 16)

                @block.gpsimd
                def _(pool):
                    nc.gpsimd.iota(lane[:], pattern=[[1, P]], base=0, channel_multiplier=0,
                                   allow_small_or_imprecise_dtypes=True).then_inc(s_iota, 1)
                    nc.gpsimd.iota(part[:], pattern=[[0, 1]], base=0, channel_multiplier=1,
                                   allow_small_or_imprecise_dtypes=True).then_inc(s_iota, 1)
                    nc.gpsimd.iota(eid[:], pattern=[[1, EJP]], base=0, channel_multiplier=EJ,
                                   allow_small_or_imprecise_dtypes=True).then_inc(s_iota, 1)
                    nc.gpsimd.iota(chunk_no[:], pattern=[[1, NCH]], base=0, channel_multiplier=0,
                                   allow_small_or_imprecise_dtypes=True).then_inc(s_iota, 1)

                @block.vector
                def _(dve):
                    v = nc.vector
                    n = [0]

                    def link(ins):
                        n[0] += 1
                        ins.then_inc(s_v, 1)
                        dve.wait_ge(s_v, n[0])

                    for a in (src_e, dst_e, typ_e):
                        link(v.memset(a[:], 0))
                    v.memset(x_sb[:, NT - 1:NTP, :], 0.0).then_inc(s_v, 1)
                    n[0] += 1
                    dve.wait_ge(s_v, n[0])
                    v.memset(tile_f[:], float(NT + 1)).then_inc(s_ms, 1)
                    v.memset(blank[:], 0).then_inc(s_const, 1)
                    dve.wait_ge(s_const, 1)
                    v.memset(blank[:, :, 2:3], -1).then_inc(s_const, 1)
                    link(v.memset(run[:], 0.0))
                    link(v.memset(ones[:], 1.0))
                    link(v.memset(onesf[:], 1.0))
                    link(v.memset(pay[:], 0))
                    dve.wait_ge(s_iota, 4)
                    link(v.tensor_scalar(ident[:], lane[:], part[:, 0:1], None, ALU.is_equal))
                    link(v.tensor_scalar(tri[:], lane[:], part[:, 0:1], None, ALU.is_gt))
                    dve.wait_ge(s_in, 16 * 8)
                    link(v.tensor_single_scalar(tmp_i[:, 0:EJP], dst_e[:], 7, ALU.logical_shift_right))
                    dve.wait_ge(s_ms, 1)
                    link(v.tensor_copy(tile_f[:, 0:EJP], tmp_i[:, 0:EJP]))
                    link(v.tensor_scalar(tmp_f[:, 0:EJP], eid[:], float(E), float(NT + 1), ALU.is_ge, ALU.mult))
                    link(v.tensor_tensor(tile_f[:, 0:EJP], tile_f[:, 0:EJP], tmp_f[:, 0:EJP], ALU.add))
                    link(v.memset(tile_f[:, EJ:EJR], float(NT + 1)))

                    def one_hot(b, s):
                        col = tile_f[:, bass.ds(b * RB, RB)]
                        return v.tensor_tensor(
                            hot[:, s], lane[:, 0:NT].unsqueeze(1).broadcast_to([P, RB, NT]),
                            col.unsqueeze(2).broadcast_to([P, RB, NT]), ALU.is_equal)

                    with dve.Fori(0, EJR // (2 * RB)) as i:
                        one_hot(2 * i, 0).then_inc(s_hot, 1)
                        one_hot(2 * i + 1, 1).then_inc(s_hot, 1)
                        dve.wait_ge(s_hot, 2 * i + 2)
                        for s in range(2):
                            dve.wait_ge(s_pre, 2 * i + (s + 1))
                            v.tensor_tensor(placed[:, s], ps[:, 2 * s, 0:RB * NT].rearrange("p (j t) -> p j t", t=NT),
                                            run[:].unsqueeze(1).broadcast_to([P, RB, NT]), ALU.add)\
                             .then_inc(s_use, 1)
                            dve.wait_ge(s_use, 6 * i + (3 * s + 1))
                            v.tensor_tensor(run[:], ps[:, 2 * s + 1, 0:NT], run[:], ALU.add).then_inc(s_use, 1)
                            v.tensor_tensor(placed[:, s], placed[:, s], hot[:, s], ALU.mult).then_inc(s_use, 1)
                            dve.wait_ge(s_use, 6 * i + (3 * s + 3))
                            v.tensor_reduce(rank[:, bass.ds((2 * i + s) * RB, RB)], placed[:, s], AX.X, ALU.add)\
                             .then_inc(s_ms, 1)
                            dve.wait_ge(s_ms, 2 * i + (s + 2))
                    link(v.tensor_scalar(nch_f[:], run[:], float(P - 1), None, ALU.add))
                    link(v.tensor_copy(nch_i[:], nch_f[:]))
                    link(v.tensor_single_scalar(nch_i[:], nch_i[:], 7, ALU.logical_shift_right))
                    link(v.tensor_copy(nch_f[:], nch_i[:]))
                    link(v.tensor_tensor_scan(ends[:], onesf[:, 0:NT], nch_f[:], 0.0, ALU.mult, ALU.add))
                    link(v.tensor_tensor(base[:], ends[:], nch_f[:], ALU.subtract))
                    v.tensor_scalar(base[:], base[:], float(P), None, ALU.mult).then_inc(s_ec, 1)
                    dve.wait_ge(s_ec, 2)
                    link(v.tensor_copy(end_col[:], ps[0:NT, 0, 0:1]))
                    v.tensor_scalar(past[:], chunk_no[:], end_col[:, 0:1], None, ALU.is_ge).then_inc(s_past, 1)
                    with dve.Fori(0, EJR // RB) as i:
                        v.tensor_tensor(
                            placed[:, 0], lane[:, 0:NT].unsqueeze(1).broadcast_to([P, RB, NT]),
                            tile_f[:, bass.ds(i * RB, RB)].unsqueeze(2).broadcast_to([P, RB, NT]),
                            ALU.is_equal).then_inc(s_use, 1)
                        dve.wait_ge(s_use, 6 * (EJR // (2 * RB)) + 2 * i + 1)
                        v.tensor_tensor(placed[:, 1], placed[:, 0],
                                        base[:].unsqueeze(1).broadcast_to([P, RB, NT]), ALU.mult).then_inc(s_use, 1)
                        dve.wait_ge(s_use, 6 * (EJR // (2 * RB)) + 2 * i + 2)
                        v.tensor_reduce(tmp_f[:, bass.ds(i * RB, RB)], placed[:, 1], AX.X, ALU.add).then_inc(s_ms, 1)
                        dve.wait_ge(s_ms, 1 + EJR // RB + i + 1)
                    w = slice(0, EJP)
                    link(v.tensor_tensor(rank[:, w], rank[:, w], tmp_f[:, w], ALU.add))
                    link(v.tensor_copy(row_i[:], rank[:, w]))
                    link(v.tensor_single_scalar(tmp_i[:, w], row_i[:], 7, ALU.logical_shift_right))
                    link(v.tensor_copy(rank[:, w], tmp_i[:, w]))
                    link(v.tensor_single_scalar(tmp_i[:, w], row_i[:], P - 1, ALU.bitwise_and))
                    link(v.tensor_copy(tmp_f[:, w], tmp_i[:, w]))
                    link(v.scalar_tensor_tensor(out=rank[:, w], in0=tmp_f[:, w], scalar=float(NCH),
                                                in1=rank[:, w], op0=ALU.mult, op1=ALU.add))
                    link(v.tensor_scalar(tmp_f[:, w], tile_f[:, w], float(NT), float(OUTSIDE), ALU.is_ge, ALU.mult))
                    link(v.tensor_tensor(rank[:, w], rank[:, w], tmp_f[:, w], ALU.add))
                    link(v.tensor_copy(row_i[:], rank[:, w]))
                    link(v.tensor_copy(rank[:, w], src_e[:]))
                    link(v.tensor_copy(tmp_f[:, w], typ_e[:]))
                    link(v.scalar_tensor_tensor(out=tmp_f[:, w], in0=rank[:, w], scalar=float(R),
                                                in1=tmp_f[:, w], op0=ALU.mult, op1=ALU.add))
                    link(v.tensor_copy(pay[:, :, 0], tmp_f[:, w]))
                    link(v.tensor_copy(pay[:, :, 1], src_e[:]))
                    link(v.tensor_single_scalar(pay[:, :, 2], dst_e[:], P - 1, ALU.bitwise_and))
                    for c in range(2):
                        h = slice(c * NCH // 2, (c + 1) * NCH // 2)
                        dve.wait_ge(s_tile, c + 1)
                        link(v.tensor_copy(chunk_tile[0:1, h], ps[0:1, 4 + c, 0:NCH // 2]))

                @block.tensor
                def _(pe):
                    with pe.Fori(0, EJR // (2 * RB)) as i:
                        for s in range(2):
                            pe.wait_ge(s_hot, 2 * i + (s + 1))
                            pre = ps[:, 2 * s, 0:RB * NT].rearrange("p (j t) -> p j t", t=NT)
                            nc.tensor.matmul(pre, tri[:], hot[:, s], start=True, stop=False)
                            for d in range(1, RB):
                                nc.tensor.matmul(pre[:, d:RB, :], ones[:], hot[:, s, 0:RB - d, :],
                                                 start=False, stop=d == RB - 1)
                            for j in range(RB):
                                last = nc.tensor.matmul(ps[:, 2 * s + 1, 0:NT], ones[:], hot[:, s, j, :],
                                                        start=j == 0, stop=j == RB - 1)
                            last.then_inc(s_pre, 1)
                    pe.wait_ge(s_ec, 1)
                    nc.tensor.matmul(ps[0:NT, 0, 0:1], ends[0:1, :], onesf[0:1, 0:1], start=True, stop=True)\
                      .then_inc(s_ec, 1)
                    pe.wait_ge(s_past, 1)
                    for c in range(2):
                        nc.tensor.matmul(ps[0:1, 4 + c, 0:NCH // 2], onesf[0:NT, 0:1],
                                         past[:, c * NCH // 2:(c + 1) * NCH // 2], start=True, stop=True)\
                          .then_inc(s_tile, 1)

            w0 = sb("w0", [P, R, D], fp32, ph)
            rf_b = sb("rf_b", [P, R * D], fp32, ph)
            y_out = sb("y_out", [P, 2, 2, 512], fp32, ph)
            xs = sb("xs0", [P, D], fp32, ph)
            xt = sb("xt0", [P, D], fp32, ph)
            st_row = sb("st_row", [P, 2, SU], i32, ph)
            st_pay = sb("st_pay", [P, 2, SU, 4], i32, ph)

            s_w = sem("weights0_in", ph)
            s_st = sem("scatter_staged", ph)
            s_sc = [sem("scattered_even", ph), sem("scattered_odd", ph)]
            s_xs = sem("x_tile_staged", ph)
            s_xtp = sem("x_tile_transposed", ph)
            s_xt = sem("x_tile_ready", ph)
            s_y = sem("y_products", ph)
            s_yc = sem("y_added", ph)
            s_yo = [sem("y_stored_even", ph), sem("y_stored_odd", ph)]
            GRP = R * D // 512
            HB = EJP // SU
            y_view = y_tab.rearrange("(t p r) d -> t p (r d)", p=P, r=R)

            with nc.Block() as block:
                @block.sync
                def _(sp):
                    sp.dma_start(w0[:], relw.rearrange("r d f -> d r f")).then_inc(s_w, 16)
                    sp.dma_start(rf_b[:], rfeat.rearrange("r d -> (r d)").unsqueeze(0).broadcast_to([P, R * D]))\
                      .then_inc(s_w, 16)
                    sp.wait_ge(s_w, 32)

                    with sp.Fori(0, NTP // 2) as i:
                        for g in range(GRP):
                            c = g % (GRP // 2)
                            sp.wait_ge(s_yc, i * (2 * GRP) + (2 * g + 2))
                            sp.dma_start(y_view[bass.ds(2 * i + g // (GRP // 2), 1), :, c * 1024:(c + 1) * 1024]
                                         .rearrange("t p w -> (t p) w"),
                                         y_out[:, g % 2].rearrange("p a w -> p (a w)"))\
                              .then_inc(s_yo[g % 2], 16)
                    for s in range(2):
                        sp.wait_ge(s_yo[s], 16 * (NTP * GRP // 4))

                @block.gpsimd
                def _(pool):
                    with pool.Fori(0, HB // 2) as i:
                        for s in range(2):
                            pool.wait_ge(s_st, i * 4 + (2 * s + 2))
                            pool.sem_inc(s_tick, 1)
                            for j in range(SU):
                                nc.gpsimd.indirect_dma_start(
                                    out=rec_tab, out_offset=bass.IndirectOffsetOnAxis(ap=st_row[:, s, j:j + 1], axis=0),
                                    in_=st_pay[:, s, j, :], in_offset=None,
                                    bounds_check=SLOTS - 1, oob_is_err=False).then_inc(s_sc[s], 16)
                    for s in range(2):
                        pool.wait_ge(s_sc[s], 16 * SU * (HB // 2))

                @block.scalar
                def _(act):
                    with act.Fori(0, NTP) as t:
                        act.wait_ge(s_xtp, t)
                        nc.scalar.activation(xs[:], x_sb[:, bass.ds(t, 1), :].rearrange("p t d -> p (t d)"),
                                             ACT.Copy).then_inc(s_xs, 1)
                        act.wait_ge(s_xtp, t + 1)
                        act.wait_ge(s_y, t * GRP)
                        nc.scalar.activation(xt[:], ps[:, 7, 0:P], ACT.Copy).then_inc(s_xt, 1)

                @block.tensor
                def _(pe):
                    pe.wait_ge(s_w, 32)
                    with pe.Fori(0, NTP // 2) as i:
                        for a in range(2):
                            pe.wait_ge(s_xs, 2 * i + (a + 1))
                            nc.tensor.transpose(ps[:, 7, 0:P], xs[:], ident[:]).then_inc(s_xtp, 1)
                            pe.wait_ge(s_xt, 2 * i + (a + 1))
                            for g in range(GRP):
                                pe.wait_ge(s_yc, i * (2 * GRP) + max(a * GRP + g - 3, 0))
                                nc.tensor.matmul(ps[:, (a * GRP + g) % 4, :], xt[:], w0[:, 4 * g:4 * g + 4, :],
                                                 start=True, stop=True).then_inc(s_y, 1)

                @block.vector
                def _(dve):
                    v = nc.vector
                    dve.wait_ge(s_w, 32)
                    stage_at = {3: 0, 13: 1}

                    def add(i, g):
                        dve.wait_ge(s_y, i * (2 * GRP) + (g + 1))
                        if g % 2 == 0:
                            d = g // 2
                            dve.wait_ge(s_yo[d % 2], i * (16 * GRP // 2) + 16 * (d // 2))
                        v.tensor_tensor(y_out[:, (g // 2) % 2, g % 2, :], ps[:, g % 4, :],
                                        rf_b[:, (g % GRP) * 512:(g % GRP + 1) * 512], ALU.add).then_inc(s_yc, 1)

                    def stage(h, s):
                        v.tensor_copy(st_row[:, s, :], row_i[:, bass.ds(h * SU, SU)]).then_inc(s_st, 1)
                        v.tensor_copy(st_pay[:, s], pay[:, bass.ds(h * SU, SU), :]).then_inc(s_st, 1)

                    stage(0, 0)
                    stage(1, 1)
                    with dve.Fori(0, NTP // 2) as i:
                        for g in range(2 * GRP):
                            add(i, g)
                            if g in stage_at:
                                s = stage_at[g]
                                dve.wait_ge(s_sc[s], (i + 1) * (16 * SU))
                                stage(2 * i + (2 + s), s)

        with Phase() as ph:
            rec = sb("rec", [P, NCH, 4], i32, ph)
            dl_t = sb("dl_t", [P, -(-NCH // P), P], bf16, ph)
            s_r = sem("records_in", ph)
            s_c = sem("records_unpacked", ph)
            s_t = sem("dl_transposed", ph)
            s_d = sem("dl_rows_ready", ph)
            s_o = sem("dl_rows_stored", ph)
            BL = -(-NCH // P)

            with nc.Block() as block:
                @block.sync
                def _(sp):
                    sp.dma_start(rec[:], rec_tab.rearrange("(p c) w -> p c w", p=P)).then_inc(s_r, 16)
                    sp.wait_ge(s_d, BL)
                    for b in range(BL):
                        rows = min(P, NCH - b * P)
                        sp.dma_start(dl_tab[b * P:b * P + rows, :], dl_t[0:rows, b, :]).then_inc(s_o, 16)
                    sp.wait_ge(s_o, 16 * BL)

                @block.vector
                def _(dve):
                    v = nc.vector
                    dve.wait_ge(s_r, 16)
                    v.tensor_copy(dl_f[:], rec[:, :, 2]).then_inc(s_c, 1)
                    v.tensor_copy(y_row[:], rec[:, :, 0]).then_inc(s_c, 1)
                    v.tensor_copy(src_row[:], rec[:, :, 1]).then_inc(s_c, 1)
                    for b in range(BL):
                        rows = min(P, NCH - b * P)
                        dve.wait_ge(s_t, b + 1)
                        v.tensor_copy(dl_t[0:rows, b, :], ps[0:rows, b, 0:P]).then_inc(s_d, 1)
                    dve.wait_ge(s_c, 3)

                @block.tensor
                def _(pe):
                    pe.wait_ge(s_c, 1)
                    for b in range(BL):
                        rows = min(P, NCH - b * P)
                        nc.tensor.transpose(ps[0:rows, b, 0:P], dl_f[:, b * P:b * P + rows], ident[:])\
                          .then_inc(s_t, 1)

        def stage_and_gather(dve, pool, table, rows, ring, st, s_stage, s_gath, s_free, width):
            def stage(q, s):
                if not isinstance(q, int) or q >= RING:
                    dve.wait_ge(s_gath[s], gathered(q, s) - 16 * CQ)
                nc.vector.tensor_copy(st[:, s, :], rows[:, bass.ds(q * CQ, CQ)]).then_inc(s_stage, 1)

            def gather(q, s):
                pool.wait_ge(s_stage, q + 1)
                if not isinstance(q, int) or q >= RING:
                    pool.wait_ge(s_free, q - (RING - 1))
                pool.sem_inc(s_tick, 1)
                for c in range(CQ):
                    nc.gpsimd.indirect_dma_start(
                        out=ring[:, s, c, 0:width], out_offset=None, in_=table,
                        in_offset=bass.IndirectOffsetOnAxis(ap=st[:, s, c:c + 1], axis=0)).then_inc(s_gath[s], 16)
            return stage, gather

        def gathered(q, s):
            if isinstance(q, int):
                return (q // RING + 1) * 16 * CQ
            return (q - s) * (16 * CQ // RING) + 16 * CQ

        def loaded(q, s):
            if isinstance(q, int):
                return (q // RING + 1) * 16
            return (q - s) * (16 // RING) + 16

        def tiles_of(engine, q):
            return nc.values_load_multi_w_load_instructions(
                chunk_tile[0:1, bass.ds(q * CQ, CQ)], engines=engine, min_val=0, max_val=NT,
                skip_runtime_bounds_check_because="the number of buckets, of NT, that ended before a chunk")[1]

        def hot_quad(q, out_ap, op=ALU.is_equal):
            return nc.vector.tensor_tensor(
                out_ap, lane[:].unsqueeze(1).broadcast_to([P, CQ, P]),
                dl_f[:, bass.ds(q * CQ, CQ)].unsqueeze(2).broadcast_to([P, CQ, P]), op)

        def project(name, ph, k, weights, width):
            xs = sb(f"xs_{name}", [P, 2, k * P], fp32, ph)
            xt = sb(f"xt_{name}", [P, 2, k * P], fp32, ph)
            s_xs = sem(f"staged_{name}", ph)
            s_tp = sem(f"transposed_{name}", ph)
            s_xt = sem(f"stationary_{name}", ph)
            s_mm = sem(f"product_{name}", ph)
            s_ev = sem(f"product_read_{name}", ph)

            def act_part(act, tile):
                with act.Fori(0, NTP // 2) as i:
                    for s in range(2):
                        act.wait_ge(s_tp, 2 * i)
                        nc.scalar.activation(xs[:, s], tile(2 * i + s), ACT.Copy).then_inc(s_xs, 1)

            def pe_part(pe):
                with pe.Fori(0, NTP // 2) as i:
                    for s in range(2):
                        pe.wait_ge(s_xs, 2 * i + (s + 1))
                        for b in range(k):
                            last = nc.tensor.transpose(ps[:, 4 + s, b * P:(b + 1) * P],
                                                       xs[:, s, b * P:(b + 1) * P], ident[:])
                        last.then_inc(s_tp, 1)
                    for s in range(2):
                        pe.wait_ge(s_xt, 2 * i + (s + 1))
                        pe.wait_ge(s_ev, 2 * i)
                        for b in range(k):
                            last = nc.tensor.matmul(ps[:, s, 0:width], xt[:, s, b * P:(b + 1) * P],
                                                    weights[:, b, :], start=b == 0, stop=b == k - 1)
                        last.then_inc(s_mm, 1)

            def dve_part(dve, read, ready=None):
                with dve.Fori(0, NTP // 2) as i:
                    for s in range(2):
                        dve.wait_ge(s_tp, 2 * i + (s + 1))
                        dve.wait_ge(s_mm, 2 * i)
                        nc.vector.tensor_copy(xt[:, s], ps[:, 4 + s, 0:k * P]).then_inc(s_xt, 1)
                    for s in range(2):
                        dve.wait_ge(s_mm, 2 * i + (s + 1))
                        if ready is not None:
                            ready(i, s)
                        read(2 * i + s, s).then_inc(s_ev, 1)
                dve.wait_ge(s_ev, NTP)

            return act_part, pe_part, dve_part

        def tile_of(big):
            return lambda t: big[:, bass.ds(t, 1), :].rearrange("p t d -> p (t d)")

        def normalizer(name, ph):
            sq = sb(f"sq_{name}", [P, NTP, D], fp32, ph)
            mean = sb(f"mean_{name}", [P, NTP], fp32, ph)
            var = sb(f"var_{name}", [P, NTP], fp32, ph)
            std = sb(f"std_{name}", [P, NTP], fp32, ph)
            s_cen = sem(f"centred_{name}", ph)
            s_sq = sem(f"squared_{name}", ph)
            s_var = sem(f"variances_{name}", ph)
            s_std = sem(f"deviations_{name}", ph)

            def dve_part(dve, link):
                v = nc.vector
                link(v.tensor_reduce(mean[:], x_sb[:], AX.X, ALU.add))
                link(v.tensor_scalar(mean[:], mean[:], 1.0 / D, None, ALU.mult))
                v.tensor_tensor(x_sb[:], x_sb[:], mean[:].unsqueeze(2).broadcast_to([P, NTP, D]),
                                ALU.subtract).then_inc(s_cen, 1)
                dve.wait_ge(s_sq, 1)
                link(v.tensor_reduce(var[:], sq[:], AX.X, ALU.add))
                v.tensor_scalar(var[:], var[:], 1.0 / D, 1e-5, ALU.mult, ALU.add).then_inc(s_var, 1)
                dve.wait_ge(s_std, 1)
                link(v.reciprocal(std[:], std[:]))
                link(v.tensor_tensor(x_sb[:], x_sb[:], std[:].unsqueeze(2).broadcast_to([P, NTP, D]), ALU.mult))

            def act_part(act):
                act.wait_ge(s_cen, 1)
                nc.scalar.activation(sq[:], x_sb[:], ACT.Square).then_inc(s_sq, 1)
                act.wait_ge(s_var, 1)
                nc.scalar.activation(std[:], var[:], ACT.Sqrt).then_inc(s_std, 1)

            return dve_part, act_part

        def linker(dve, s, base=0):
            count = [0]

            def link(ins):
                count[0] += 1
                ins.then_inc(s, 1)
                dve.wait_ge(s, base + count[0])
            return link

        acc0 = ctx.enter_context(ExitStack())
        acc = sb("acc", [P, NTP, HEADS * F1 + HEADS], fp32, acc0)

        with Phase() as ph:
            W = D + 1
            ring = sb("ring_0", [P, RING, CQ, W], fp32, ph)
            st = sb("st_0", [P, RING, CQ], i32, ph)
            hots = sb("hots_0", [P, RING, CQ, P], fp32, ph)
            s_ini = sem("acc_cleared_0", ph)
            s_stage = sem("rows_staged_0", ph)
            s_gath = [sem(f"gathered_0_{s}", ph) for s in range(RING)]
            s_hot = sem("hot_0", ph)
            s_sum = sem("summed_0", ph)
            s_acc = sem("added_0", ph)

            with nc.Block() as block:
                @block.gpsimd
                def _(pool):
                    pool.wait_ge(s_ini, 2)
                    _, gather = stage_and_gather(None, pool, y_tab, y_row, ring, st, s_stage, s_gath, s_sum, D)
                    sweep(pool, [(0, gather)])

                @block.vector
                def _(dve):
                    nc.vector.memset(acc[:], 0.0).then_inc(s_ini, 1)
                    nc.vector.memset(ring[:], 1.0).then_inc(s_ini, 1)
                    dve.wait_ge(s_ini, 2)
                    stage, _ = stage_and_gather(dve, None, y_tab, y_row, ring, st, s_stage, s_gath, s_sum, D)

                    def hot(q, s):
                        if not isinstance(q, int) or q >= RING:
                            dve.wait_ge(s_sum, q - (RING - 1))
                        hot_quad(q, hots[:, s]).then_inc(s_hot, 1)

                    def add(q, s):
                        tiles = tiles_of(DVE_ENGINE, q)
                        dve.wait_ge(s_sum, q + 1)
                        if not isinstance(q, int) or q >= 1:
                            dve.wait_ge(s_acc, q * CQ)
                        for c in range(CQ):
                            a = acc[:, bass.ds(tiles[c], 1), 0:W].rearrange("p t w -> p (t w)")
                            ins = nc.vector.tensor_tensor(a, ps[:, (s % 2) * CQ + c, 0:W], a, ALU.add)
                            ins.then_inc(s_acc, 1)
                            if c < CQ - 1:
                                dve.wait_ge(s_acc, q * CQ + (c + 1))
                    sweep(dve, [(3, stage), (1, hot), (0, add)])

                @block.tensor
                def _(pe):
                    def total(q, s):
                        pe.wait_ge(s_hot, q + 1)
                        pe.wait_ge(s_gath[s], gathered(q, s))
                        if not isinstance(q, int) or q >= 2:
                            pe.wait_ge(s_acc, (q - 1) * CQ)
                        for c in range(CQ):
                            last = nc.tensor.matmul(ps[:, (s % 2) * CQ + c, 0:W], hots[:, s, c, :], ring[:, s, c, :],
                                                    start=True, stop=True)
                        last.then_inc(s_sum, 1)
                    sweep(pe, [(0, total)])

        with Phase() as ph:
            h0 = sb("h0", [P, NTP, D], fp32, ph)
            wl = sb("wl", [P, 1, D], fp32, ph)
            deg = sb("deg", [P, NTP], fp32, ph)
            s_w = sem("loop_weight_in", ph)
            s_l = sem("arithmetic_0", ph)
            s_deg = sem("degrees_0", ph)
            s_rt = sem("degree_roots_0", ph)
            s_h = sem("h_ready_0", ph)
            act_p, pe_p, dve_p = project("l0", ph, 1, wl, D)
            ln_dve, ln_act = normalizer("l0", ph)

            with nc.Block() as block:
                @block.sync
                def _(sp):
                    sp.dma_start(wl[:, 0, :], loopw).then_inc(s_w, 16)
                    sp.wait_ge(s_w, 16)

                @block.vector
                def _(dve):
                    v = nc.vector
                    link = linker(dve, s_l)
                    v.tensor_scalar(deg[:], acc[:, :, D], 1.0, None, ALU.max).then_inc(s_deg, 1)
                    dve.wait_ge(s_rt, 1)
                    link(v.reciprocal(deg[:], deg[:]))
                    v.tensor_tensor(h0[:], acc[:, :, 0:D], deg[:].unsqueeze(2).broadcast_to([P, NTP, D]),
                                    ALU.mult).then_inc(s_h, 1)
                    dve.wait_ge(s_h, 1)

                    def read(t, s):
                        a = acc[:, bass.ds(t, 1), 0:D].rearrange("p t d -> p (t d)")
                        return v.tensor_tensor(a, ps[:, s, 0:D], tile_of(h0)(t), ALU.add)
                    dve_p(dve, read)
                    link(v.scalar_tensor_tensor(out=x_sb[:], in0=acc[:, :, 0:D], scalar=0.0, in1=x_sb[:],
                                                op0=ALU.max, op1=ALU.add))
                    ln_dve(dve, link)

                @block.scalar
                def _(act):
                    act.wait_ge(s_deg, 1)
                    nc.scalar.activation(deg[:], deg[:], ACT.Sqrt).then_inc(s_rt, 1)
                    act.wait_ge(s_h, 1)
                    act_p(act, tile_of(h0))
                    ln_act(act)

                @block.tensor
                def _(pe):
                    pe.wait_ge(s_w, 16)
                    pe_p(pe)

        def attention_tables(name, ph, f, w_in, s_in, d_in, skip_in, t_tab, a_tab, a_src, a_dst, skip):
            hf = HEADS * f
            wide = hf + 2 * HEADS + (D if skip_in is not None else 0)
            wts = sb(f"wts_{name}", [P, 1, wide], fp32, ph)
            att = sb(f"att_{name}", [P, 2, hf], fp32, ph)
            prod = sb(f"attw_{name}", [P, 2, hf], fp32, ph)
            rows = sb(f"rows_{name}", [P, 2, hf + HEADS], fp32, ph)
            s_w = sem(f"weights_in_{name}", ph)
            s_l = sem(f"arithmetic_{name}", ph)
            s_wt = sem(f"weights_ready_{name}", ph)
            s_rows = sem(f"rows_ready_{name}", ph)
            s_all = sem(f"all_tiles_{name}", ph)
            s_st = [sem(f"rows_stored_even_{name}", ph), sem(f"rows_stored_odd_{name}", ph)]
            s_as = sem(f"scores_stored_{name}", ph)
            act_p, pe_p, dve_p = project(name, ph, 1, wts, wide)
            tab = t_tab.rearrange("(t p) w -> t p w", p=P)

            with nc.Block() as block:
                @block.sync
                def _(sp):
                    sp.dma_start(wts[:, 0, 0:hf], w_in).then_inc(s_w, 16)
                    sp.dma_start(att[:, 0, :], s_in.unsqueeze(0).broadcast_to([P, hf])).then_inc(s_w, 16)
                    sp.dma_start(att[:, 1, :], d_in.unsqueeze(0).broadcast_to([P, hf])).then_inc(s_w, 16)
                    if skip_in is not None:
                        sp.dma_start(wts[:, 0, hf + 2 * HEADS:wide], skip_in).then_inc(s_w, 16)
                    with sp.Fori(0, NTP // 2) as i:
                        for s in range(2):
                            sp.wait_ge(s_rows, 2 * i + (s + 1))
                            sp.dma_start(tab[bass.ds(2 * i + s, 1), :, :].rearrange("t p w -> (t p) w"),
                                         rows[:, s, :]).then_inc(s_st[s], 16)
                    sp.wait_ge(s_all, 1)
                    sp.dma_start(a_tab.rearrange("(t p) h -> p t h", p=P), a_src[:]).then_inc(s_as, 16)
                    sp.wait_ge(s_as, 16)
                    for s in range(2):
                        sp.wait_ge(s_st[s], 16 * (NTP // 2))

                @block.vector
                def _(dve):
                    v = nc.vector
                    link = linker(dve, s_l)
                    dve.wait_ge(s_w, 48 if skip_in is None else 64)
                    link(v.tensor_tensor(prod[:], att[:], wts[:, 0:1, 0:hf].broadcast_to([P, 2, hf]), ALU.mult))
                    v.tensor_reduce(wts[:, 0, hf:hf + 2 * HEADS],
                                    prod[:].rearrange("p a (h f) -> p (a h) f", f=f), AX.X, ALU.add)\
                     .then_inc(s_wt, 1)

                    def free(i, s):
                        dve.wait_ge(s_st[s], i * 16)

                    def read(t, s):
                        v.tensor_copy(rows[:, s, :], ps[:, s, 0:hf + HEADS]).then_inc(s_rows, 1)
                        v.tensor_copy(a_src[:, bass.ds(t, 1), :].rearrange("p t h -> p (t h)"),
                                      ps[:, s, hf:hf + HEADS])
                        if skip is not None:
                            v.tensor_copy(skip[:, bass.ds(t, 1), :].rearrange("p t h -> p (t h)"),
                                          ps[:, s, hf + 2 * HEADS:wide])
                        return v.tensor_copy(a_dst[:, bass.ds(t, 1), :].rearrange("p t h -> p (t h)"),
                                             ps[:, s, hf + HEADS:hf + 2 * HEADS])
                    dve_p(dve, read, free)
                    v.nop().then_inc(s_all, 1)

                @block.scalar
                def _(act):
                    act_p(act, tile_of(x_sb))

                @block.tensor
                def _(pe):
                    pe.wait_ge(s_wt, 1)
                    pe_p(pe)

        def source_maximum(name, a_tab, most):
            with Phase() as ph:
                ring = sb(f"ring_{name}", [P, RING, CQ, HEADS], fp32, ph)
                st = sb(f"st_{name}", [P, RING, CQ], i32, ph)
                others = sb(f"others_{name}", [P, RING, CQ, P], bf16, ph)
                lines = sb(f"lines_{name}", [CQ * HEADS, RING, P], fp32, ph)
                pick = sb(f"pick_{name}", [CQ * HEADS, CQ * HEADS, P], fp32, ph)
                far = sb(f"far_{name}", [P, HEADS, P], bf16, ph)
                high = sb(f"high_{name}", [P, CQ, HEADS], fp32, ph)
                s_ini = sem(f"constants_{name}", ph)
                s_stage = sem(f"rows_staged_{name}", ph)
                s_gath = [sem(f"gathered_{name}_{s}", ph) for s in range(RING)]
                s_turn = sem(f"turned_{name}", ph)
                s_line = sem(f"lines_{name}_ready", ph)
                s_oth = sem(f"others_{name}_made", ph)
                s_spread = sem(f"spread_{name}", ph)
                s_red = sem(f"reduced_{name}", ph)
                s_max = sem(f"maxima_{name}", ph)

                with nc.Block() as block:
                    @block.gpsimd
                    def _(pool):
                        _, gather = stage_and_gather(None, pool, a_tab, src_row, ring, st, s_stage, s_gath,
                                                     s_turn, HEADS)
                        sweep(pool, [(0, gather)])

                    @block.vector
                    def _(dve):
                        v = nc.vector
                        v.memset(most[:], -BIG).then_inc(s_ini, 1)
                        v.tensor_scalar(pick[:], lane[0:CQ * HEADS, 0:CQ * HEADS].unsqueeze(2)
                                        .broadcast_to([CQ * HEADS, CQ * HEADS, P]),
                                        part[0:CQ * HEADS, 0:1], None, ALU.is_equal).then_inc(s_ini, 1)
                        v.tensor_scalar(far[:], ident[:].unsqueeze(1).broadcast_to([P, HEADS, P]), -BIG, None,
                                        ALU.mult).then_inc(s_ini, 1)
                        dve.wait_ge(s_ini, 3)
                        stage, _ = stage_and_gather(dve, None, a_tab, src_row, ring, st, s_stage, s_gath,
                                                    s_turn, HEADS)

                        def other(q, s):
                            if not isinstance(q, int) or q >= RING:
                                dve.wait_ge(s_spread, (q - RING) * CQ + CQ)
                            hot_quad(q, others[:, s], ALU.not_equal).then_inc(s_oth, 1)

                        def top(q, s):
                            tiles = tiles_of(DVE_ENGINE, q)
                            for c in range(CQ):
                                dve.wait_ge(s_spread, q * CQ + (c + 1))
                                if not isinstance(q, int) or q >= 1:
                                    dve.wait_ge(s_max, q * CQ + c)
                                elif c:
                                    dve.wait_ge(s_max, c)
                                v.tensor_reduce(high[:, c, :], ps[:, c, :].rearrange("p (h e) -> p h e", e=P),
                                                AX.X, ALU.max).then_inc(s_red, 1)
                                dve.wait_ge(s_red, q * CQ + (c + 1))
                                m = most[:, bass.ds(tiles[c], 1), :].rearrange("p t h -> p (t h)")
                                v.tensor_tensor(m, high[:, c, :], m, ALU.max).then_inc(s_max, 1)
                        sweep(dve, [(3, stage), (1, other), (0, top)])

                    @block.scalar
                    def _(act):
                        def line(q, s):
                            act.wait_ge(s_turn, q + 1)
                            if not isinstance(q, int) or q >= RING:
                                act.wait_ge(s_spread, (q - RING) * CQ + CQ)
                            nc.scalar.activation(lines[:, s, :], ps[0:CQ * HEADS, 4 + s % 2, 0:P], ACT.Copy)\
                              .then_inc(s_line, 1)
                        sweep(act, [(0, line)])

                    @block.tensor
                    def _(pe):
                        pe.wait_ge(s_ini, 3)

                        def turn(q, s):
                            pe.wait_ge(s_gath[s], gathered(q, s))
                            if not isinstance(q, int) or q >= 2:
                                pe.wait_ge(s_line, q - 1)
                            nc.tensor.transpose(ps[0:CQ * HEADS, 4 + s % 2, 0:P],
                                                ring[:, s].rearrange("p c h -> p (c h)"), ident[:])\
                              .then_inc(s_turn, 1)

                        def spread(q, s):
                            pe.wait_ge(s_line, q + 1)
                            pe.wait_ge(s_oth, q + 1)
                            for c in range(CQ):
                                if not isinstance(q, int) or q >= 1:
                                    pe.wait_ge(s_red, (q - 1) * CQ + (c + 1))
                                for h in range(HEADS):
                                    nc.tensor.matmul(ps[:, c, h * P:(h + 1) * P], pick[:, c * HEADS + h, :],
                                                     lines[:, s, :], start=h == 0, stop=False)
                                nc.tensor.matmul(ps[:, c, :], others[:, s, c, :],
                                                 far[:].rearrange("p h e -> p (h e)"), start=False, stop=True)\
                                  .then_inc(s_spread, 1)
                        sweep(pe, [(1, turn), (0, spread)])

        def split_bf16(link, exact, parts, rest):
            v = nc.vector
            link(v.tensor_copy(parts(0), exact))
            link(v.tensor_tensor(rest, exact, parts(0), ALU.subtract))
            link(v.tensor_copy(parts(1), rest))
            link(v.tensor_tensor(rest, rest, parts(1), ALU.subtract))
            link(v.tensor_copy(parts(2), rest))

        def target_rows(name, ph, a_src, a_dst, most, everywhere, exp_n, own):
            both = sb(f"both_{name}", [P, NTP, 2 * HEADS], fp32, ph)
            rest = sb(f"rest_{name}", [P, NTP, 2 * HEADS], fp32, ph)
            mine = sb(f"mine_{name}", [P, 1], fp32, ph)
            whole = sb(f"whole_{name}", [P, 1], fp32, ph)
            s_l = sem(f"arithmetic_{name}", ph)
            s_m = sem(f"own_maximum_{name}", ph)
            s_g = sem(f"global_maximum_{name}", ph)

            with nc.Block() as block:
                @block.vector
                def _(dve):
                    v = nc.vector
                    link = linker(dve, s_l)
                    link(v.tensor_copy(both[:, :, 0:HEADS], a_dst[:]))
                    if own is not None:
                        link(v.tensor_tensor(most[:], most[:], a_src[:], ALU.max))
                        link(v.tensor_tensor(own[:], a_src[:], a_dst[:], ALU.add))
                        link(v.scalar_tensor_tensor(out=own[:], in0=own[:], scalar=0.2, in1=own[:],
                                                    op0=ALU.mult, op1=ALU.max))
                    link(v.tensor_tensor(most[:], most[:], a_dst[:], ALU.add))
                    m = both[:, :, HEADS:2 * HEADS]
                    link(v.scalar_tensor_tensor(out=m, in0=most[:], scalar=0.2, in1=most[:],
                                                op0=ALU.mult, op1=ALU.max))
                    if everywhere:
                        v.tensor_reduce(mine[:], m, AX.XY, ALU.max).then_inc(s_m, 1)
                        dve.wait_ge(s_g, 1)
                        link(v.memset(m, 0.0))
                        link(v.tensor_scalar(m, m, whole[:, 0:1], None, ALU.add))
                    if own is not None:
                        v.tensor_tensor(own[:], own[:], m, ALU.subtract).then_inc(s_m, 1)
                    split_bf16(link, both[:], lambda k: exp_n[:, :, k, :], rest[:])

                @block.scalar
                def _(act):
                    if own is not None:
                        act.wait_ge(s_m, 1)
                        nc.scalar.activation(own[:], own[:], ACT.Exp).then_inc(s_g, 1)

                @block.gpsimd
                def _(pool):
                    if everywhere:
                        pool.wait_ge(s_m, 1)
                        nc.gpsimd.partition_all_reduce(whole[:], mine[:], P, bass.bass_isa.ReduceOp.max)\
                          .then_inc(s_g, 1)

        def load_targets(sp, q, s, dl_b, s_dl, s_oht, base=0, dl_base=0):
            if not isinstance(q, int) or q >= RING:
                sp.wait_ge(s_oht, base + (q - (RING - 1)))
            sp.dma_start(dl_b[:, s, :], dl_tab.rearrange("(q c) e -> q (c e)", c=CQ)[bass.ds(q, 1), :]
                         .broadcast_to([P, CQ * P])).then_inc(s_dl[s], 16)

        def attend(name, f, t_tab, exp_n, own):
            hf = HEADS * f
            W = hf + HEADS
            with Phase() as ph:
                ring = sb(f"ring_{name}", [P, RING, CQ, W], fp32, ph)
                msg = sb(f"msg_{name}", [P, RING, CQ, W], fp32, ph)
                st = sb(f"st_{name}", [P, RING, CQ], i32, ph)
                hots = sb(f"hots_{name}", [P, RING, CQ, P], fp32, ph)
                ohts = sb(f"ohts_{name}", [P, RING, CQ, P], bf16, ph)
                dl_b = sb(f"dl_b_{name}", [P, RING, CQ * P], bf16, ph)
                sc = sb(f"sc_{name}", [P, RING, CQ, HEADS], fp32, ph)
                s_ini = sem(f"acc_begun_{name}", ph)
                s_rows = sem(f"own_rows_{name}", ph)
                s_stage = sem(f"rows_staged_{name}", ph)
                s_gath = [sem(f"gathered_{name}_{s}", ph) for s in range(RING)]
                s_dl = [sem(f"targets_{name}_{s}", ph) for s in range(RING)]
                s_hot = sem(f"hot_{name}", ph)
                s_oht = sem(f"hot_transposed_{name}", ph)
                s_exp = sem(f"expanded_{name}", ph)
                s_s = sem(f"scores_{name}", ph)
                s_e = sem(f"exponentials_{name}", ph)
                s_msg = sem(f"messages_{name}", ph)
                s_sum = sem(f"summed_{name}", ph)
                s_acc = sem(f"added_{name}", ph)

                def sums(c):
                    return ps[:, c, 0:W]

                with nc.Block() as block:
                    @block.sync
                    def _(sp):
                        if own is not None:
                            sp.dma_start(acc[:, :, 0:W], t_tab.rearrange("(t p) w -> p t w", p=P)).then_inc(s_rows, 16)
                        sweep(sp, [(0, lambda q, s: load_targets(sp, q, s, dl_b, s_dl, s_oht))])

                    @block.gpsimd
                    def _(pool):
                        _, gather = stage_and_gather(None, pool, t_tab, src_row, ring, st, s_stage, s_gath,
                                                     s_msg, W)
                        sweep(pool, [(0, gather)])

                    @block.vector
                    def _(dve):
                        v = nc.vector
                        if own is None:
                            v.memset(acc[:], 0.0).then_inc(s_ini, 1)
                            dve.wait_ge(s_ini, 1)
                        else:
                            dve.wait_ge(s_rows, 16)
                            a = acc[:, :, 0:hf].rearrange("p t (h f) -> p t h f", f=f)
                            v.tensor_tensor(a, a, own[:].unsqueeze(3).broadcast_to([P, NTP, HEADS, f]), ALU.mult)\
                             .then_inc(s_ini, 1)
                            v.tensor_copy(acc[:, :, hf:W], own[:]).then_inc(s_ini, 1)
                            dve.wait_ge(s_ini, 2)
                        stage, _ = stage_and_gather(dve, None, t_tab, src_row, ring, st, s_stage, s_gath,
                                                    s_msg, W)

                        def hot(q, s):
                            dve.wait_ge(s_dl[s], loaded(q, s))
                            if not isinstance(q, int) or q >= RING:
                                dve.wait_ge(s_exp, q - (RING - 1))
                                dve.wait_ge(s_sum, q - (RING - 1))
                            v.tensor_scalar(ohts[:, s].rearrange("p c e -> p (c e)"), dl_b[:, s, :], part[:, 0:1],
                                            None, ALU.is_equal).then_inc(s_oht, 1)
                            hot_quad(q, hots[:, s]).then_inc(s_hot, 1)

                        def score(q, s):
                            dve.wait_ge(s_gath[s], gathered(q, s))
                            dve.wait_ge(s_exp, q + 1)
                            if not isinstance(q, int) or q >= RING:
                                dve.wait_ge(s_e, q - (RING - 1))
                            e = ps[:, 6 + s % 2, 0:CQ * 2 * HEADS]\
                                .rearrange("p (c w) -> p c w", c=CQ)
                            v.tensor_tensor(sc[:, s], ring[:, s, :, hf:W], e[:, :, 0:HEADS], ALU.add)\
                             .then_inc(s_s, 1)
                            dve.wait_ge(s_s, q * 4 + 1)
                            v.scalar_tensor_tensor(out=sc[:, s], in0=sc[:, s], scalar=0.2, in1=sc[:, s],
                                                   op0=ALU.mult, op1=ALU.max).then_inc(s_s, 1)
                            dve.wait_ge(s_s, q * 4 + 2)
                            v.tensor_tensor(sc[:, s], sc[:, s], e[:, :, HEADS:2 * HEADS], ALU.subtract)\
                             .then_inc(s_s, 1)
                            dve.wait_ge(s_s, q * 4 + 3)
                            v.tensor_scalar(sc[:, s], sc[:, s], 0.0, None, ALU.min).then_inc(s_s, 1)

                        def message(q, s):
                            dve.wait_ge(s_e, q + 1)
                            if not isinstance(q, int) or q >= RING:
                                dve.wait_ge(s_sum, q - (RING - 1))
                            v.tensor_tensor(
                                msg[:, s, :, 0:hf].rearrange("p c (h f) -> p c h f", f=f),
                                ring[:, s, :, 0:hf].rearrange("p c (h f) -> p c h f", f=f),
                                msg[:, s, :, hf:W].unsqueeze(3).broadcast_to([P, CQ, HEADS, f]),
                                ALU.mult).then_inc(s_msg, 1)

                        def add(q, s):
                            tiles = tiles_of(DVE_ENGINE, q)
                            for c in range(CQ):
                                dve.wait_ge(s_sum, q + 1)
                                if not isinstance(q, int) or q * CQ + c >= 1:
                                    dve.wait_ge(s_acc, q * CQ + c)
                                a = acc[:, bass.ds(tiles[c], 1), 0:W].rearrange("p t w -> p (t w)")
                                v.tensor_tensor(a, sums(c), a, ALU.add).then_inc(s_acc, 1)
                        sweep(dve, [(3, stage), (2, hot), (1, score), (0, message), (-1, add)])

                    @block.scalar
                    def _(act):
                        def exponential(q, s):
                            act.wait_ge(s_s, q * 4 + 4)
                            if not isinstance(q, int) or q >= RING:
                                act.wait_ge(s_sum, q - (RING - 1))
                            nc.scalar.activation(msg[:, s, :, hf:W], sc[:, s], ACT.Exp).then_inc(s_e, 1)
                        sweep(act, [(0, exponential)])

                    @block.tensor
                    def _(pe):
                        def expand(q, s):
                            tiles = tiles_of(PE_ENGINE, q)
                            pe.wait_ge(s_oht, q + 1)
                            if not isinstance(q, int) or q >= 2:
                                pe.wait_ge(s_s, (q - 2) * 4 + 4)
                            for c in range(CQ):
                                o = c * 2 * HEADS
                                for k in range(3):
                                    last = nc.tensor.matmul(
                                        ps[:, 6 + s % 2, o:o + 2 * HEADS], ohts[:, s, c, :],
                                        exp_n[:, bass.ds(tiles[c], 1), k, :].rearrange("p t w -> p (t w)"),
                                        start=k == 0, stop=k == 2)
                            last.then_inc(s_exp, 1)

                        def total(q, s):
                            pe.wait_ge(s_msg, q + 1)
                            pe.wait_ge(s_hot, q + 1)
                            for c in range(CQ):
                                if not isinstance(q, int) or q >= 1:
                                    pe.wait_ge(s_acc, (q - 1) * CQ + (c + 1))
                                last = nc.tensor.matmul(sums(c), hots[:, s, c, :], msg[:, s, c, :],
                                                        start=True, stop=True)
                            last.then_inc(s_sum, 1)
                        sweep(pe, [(2, expand), (0, total)])

        with Phase() as l1:
            a_src = sb("a_src1", [P, NTP, HEADS], fp32, l1)
            a_dst = sb("a_dst1", [P, NTP, HEADS], fp32, l1)
            most = sb("most1", [P, NTP, HEADS], fp32, l1)
            own = sb("own1", [P, NTP, HEADS], fp32, l1)
            exp_n = sb("exp_n1", [P, NTP, 3, 2 * HEADS], bf16, l1)
            with Phase() as ph:
                attention_tables("t1", ph, F1, w1, att_s.rearrange("h f -> (h f)"), att_d.rearrange("h f -> (h f)"),
                                 None, t1_tab, a1_tab, a_src, a_dst, None)
            source_maximum("m1", a1_tab, most)
            with Phase() as ph:
                target_rows("n1", ph, a_src, a_dst, most, False, exp_n, own)
            attend("e1", F1, t1_tab, exp_n, own)

        with Phase() as ph:
            HF = HEADS * F1
            g1 = sb("g1", [P, NTP, HF], fp32, ph)
            wf = sb("wf", [P, 2, D], fp32, ph)
            b_b = sb("b1_b", [P, HF], fp32, ph)
            fb_b = sb("fb_b", [P, D], fp32, ph)
            den = sb("den1", [P, NTP, HEADS], fp32, ph)
            s_w = sem("fc_in", ph)
            s_l = sem("arithmetic_f1", ph)
            s_g = sem("g_ready", ph)
            s_b = sem("bias_added_1", ph)
            act_p, pe_p, dve_p = project("f1", ph, 2, wf, D)
            with nc.Block() as block:
                @block.sync
                def _(sp):
                    sp.dma_start(wf[:], fcw.rearrange("(k d) n -> d k n", d=P)).then_inc(s_w, 16)
                    sp.dma_start(b_b[:], bias1.unsqueeze(0).broadcast_to([P, HF])).then_inc(s_w, 16)
                    sp.dma_start(fb_b[:], fcb.unsqueeze(0).broadcast_to([P, D])).then_inc(s_w, 16)
                    sp.wait_ge(s_w, 48)

                @block.vector
                def _(dve):
                    v = nc.vector
                    link = linker(dve, s_l)
                    dve.wait_ge(s_w, 48)
                    link(v.reciprocal(den[:], acc[:, :, HF:HF + HEADS]))
                    link(v.tensor_tensor(g1[:].rearrange("p t (h f) -> p t h f", f=F1),
                                         acc[:, :, 0:HF].rearrange("p t (h f) -> p t h f", f=F1),
                                         den[:].unsqueeze(3).broadcast_to([P, NTP, HEADS, F1]), ALU.mult))
                    link(v.tensor_tensor(g1[:], g1[:], b_b[:].unsqueeze(1).broadcast_to([P, NTP, HF]), ALU.add))
                    v.tensor_scalar(g1[:], g1[:], 0.0, None, ALU.max).then_inc(s_g, 1)
                    v.tensor_tensor(x_sb[:], x_sb[:], fb_b[:].unsqueeze(1).broadcast_to([P, NTP, D]), ALU.add)\
                     .then_inc(s_b, 1)
                    dve.wait_ge(s_b, 1)

                    def read(t, s):
                        return v.tensor_tensor(tile_of(x_sb)(t), ps[:, s, 0:D], tile_of(x_sb)(t), ALU.add)
                    dve_p(dve, read)

                @block.scalar
                def _(act):
                    act.wait_ge(s_g, 1)
                    act_p(act, tile_of(g1))

                @block.tensor
                def _(pe):
                    pe.wait_ge(s_w, 48)
                    pe_p(pe)

        def normalize_block(name):
            with Phase() as ph:
                ln_dve, ln_act = normalizer(name, ph)
                s_l = sem(f"arithmetic_{name}", ph)
                with nc.Block() as block:
                    @block.vector
                    def _(dve):
                        ln_dve(dve, linker(dve, s_l))

                    @block.scalar
                    def _(act):
                        ln_act(act)

        normalize_block("ln1")

        with Phase() as l2:
            a_src = sb("a_src2", [P, NTP, HEADS], fp32, l2)
            a_dst = sb("a_dst2", [P, NTP, HEADS], fp32, l2)
            most = sb("most2", [P, NTP, HEADS], fp32, l2)
            exp_n = sb("exp_n2", [P, NTP, 3, 2 * HEADS], bf16, l2)
            skip = sb("skip2", [P, NTP, D], fp32, l2)
            with Phase() as ph:
                attention_tables("t2", ph, F2, wproj, sc_s.rearrange("a h f -> (a h f)"),
                                 sc_t.rearrange("a h f -> (a h f)"), wskip, t2_tab, a2_tab, a_src, a_dst, skip)
            source_maximum("m2", a2_tab, most)
            with Phase() as ph:
                target_rows("n2", ph, a_src, a_dst, most, True, exp_n, None)
            attend("e2", F2, t2_tab, exp_n, None)

            with Phase() as ph:
                b_b = sb("b2_b", [P, D], fp32, ph)
                low = sb("low2", [P, NTP, D], fp32, ph)
                den = sb("den2", [P, NTP, HEADS], fp32, ph)
                s_w = sem("bias2_in", ph)
                s_l = sem("arithmetic_f2", ph)
                s_low = sem("negatives_2", ph)
                s_ex = sem("exponentials_f2", ph)
                with nc.Block() as block:
                    @block.sync
                    def _(sp):
                        sp.dma_start(b_b[:], bias2.unsqueeze(0).broadcast_to([P, D])).then_inc(s_w, 16)
                        sp.wait_ge(s_w, 16)

                    @block.vector
                    def _(dve):
                        v = nc.vector
                        link = linker(dve, s_l)
                        dve.wait_ge(s_w, 16)
                        link(v.tensor_scalar(den[:], acc[:, :, D:D + HEADS], 1e-16, None, ALU.add))
                        link(v.reciprocal(den[:], den[:]))
                        a = acc[:, :, 0:D]
                        link(v.tensor_tensor(a.rearrange("p t (h f) -> p t h f", f=F2),
                                             a.rearrange("p t (h f) -> p t h f", f=F2),
                                             den[:].unsqueeze(3).broadcast_to([P, NTP, HEADS, F2]), ALU.mult))
                        link(v.tensor_tensor(a, a, skip[:], ALU.add))
                        link(v.tensor_tensor(a, a, b_b[:].unsqueeze(1).broadcast_to([P, NTP, D]), ALU.add))
                        v.tensor_scalar(low[:], a, 0.0, None, ALU.min).then_inc(s_low, 1)
                        link(v.scalar_tensor_tensor(out=x_sb[:], in0=a, scalar=0.0, in1=x_sb[:],
                                                    op0=ALU.max, op1=ALU.add))
                        dve.wait_ge(s_ex, 1)
                        link(v.scalar_tensor_tensor(out=x_sb[:], in0=low[:], scalar=-1.0, in1=x_sb[:],
                                                    op0=ALU.add, op1=ALU.add))

                    @block.scalar
                    def _(act):
                        act.wait_ge(s_low, 1)
                        nc.scalar.activation(low[:], low[:], ACT.Exp).then_inc(s_ex, 1)

        normalize_block("ln2")
        acc0.close()

        with Phase() as l3:
            unit = sb("unit", [P, NTP, D], fp32, l3)
            u_sum = sb("u_sum", [P, NTP, D], fp32, l3)
            u_sq = sb("u_sq", [P, NTP, D], fp32, l3)
            u_split = sb("u_split", [P, NTP, 3, D], bf16, l3)
            nrm = sb("nrm", [P, NTP * CAPS], fp32, l3)
            def capsule_norm(dve, link, src, dst, s_from, s_to, base):
                v = nc.vector
                dve.wait_ge(s_to, base + 1)
                link(v.tensor_reduce(nrm[:], u_sq[:].rearrange("p t (k c) -> p (t k) c", c=CD), AX.X, ALU.add))
                nc.vector.nop().then_inc(s_from, 1)
                dve.wait_ge(s_to, base + 2)
                link(v.tensor_scalar(nrm[:], nrm[:], 1e-12, None, ALU.max))
                link(v.reciprocal(nrm[:], nrm[:]))
                link(v.tensor_tensor(dst[:].rearrange("p t (k c) -> p (t k) c", c=CD),
                                     src[:].rearrange("p t (k c) -> p (t k) c", c=CD),
                                     nrm[:].unsqueeze(2).broadcast_to([P, NTP * CAPS, CD]), ALU.mult))

            with Phase() as ph:
                s_l = sem("arithmetic_u0", ph)
                s_f = sem("square_sums_u0", ph)
                s_t = sem("squares_and_roots_u0", ph)
                s_u = sem("unit_ready", ph)
                s_o = sem("unit_stored", ph)
                with nc.Block() as block:
                    @block.vector
                    def _(dve):
                        v = nc.vector
                        link = linker(dve, s_l)
                        capsule_norm(dve, link, x_sb, unit, s_f, s_t, 0)
                        v.nop().then_inc(s_u, 1)
                        split_bf16(link, unit[:], lambda k: u_split[:, :, k, :], u_sq[:])

                    @block.scalar
                    def _(act):
                        nc.scalar.activation(u_sq[:], x_sb[:], ACT.Square).then_inc(s_t, 1)
                        act.wait_ge(s_f, 1)
                        nc.scalar.activation(nrm[:], nrm[:], ACT.Sqrt).then_inc(s_t, 1)

                    @block.sync
                    def _(sp):
                        sp.wait_ge(s_u, 1)
                        sp.dma_start(x3_tab.rearrange("(t p) d -> p t d", p=P), unit[:]).then_inc(s_o, 16)
                        sp.wait_ge(s_o, 16)

            def route(name, rounds, gathers):
                with Phase() as ph:
                    z = sb(f"z_{name}", [P, RING, CQ * D], fp32, ph)
                    msg = sb(f"msg_{name}", [P, RING, CQ * D], fp32, ph)
                    prod = sb(f"prod_{name}", [P, 2, CQ * D], fp32, ph)
                    st = sb(f"st_{name}", [P, RING, CQ], i32, ph)
                    hots = sb(f"hots_{name}", [P, RING, CQ, P], fp32, ph)
                    ohts = sb(f"ohts_{name}", [P, RING, CQ, P], bf16, ph)
                    dl_b = sb(f"dl_b_{name}", [P, RING, CQ * P], bf16, ph)
                    dot = sb(f"dot_{name}", [P, RING, CQ * CAPS], fp32, ph)
                    ex = sb(f"ex_{name}", [P, RING, CQ * CAPS], fp32, ph)
                    tot = sb(f"tot_{name}", [P, RING, CQ], fp32, ph)
                    s_stage = sem(f"rows_staged_{name}", ph)
                    s_z = [sem(f"sources_{name}_{s}", ph) for s in range(RING)]
                    s_zst = [sem(f"sources_stored_{name}_{s}", ph) for s in range(RING)]
                    s_dl = [sem(f"targets_{name}_{s}", ph) for s in range(RING)]
                    s_hot = sem(f"hot_{name}", ph)
                    s_oht = sem(f"hot_transposed_{name}", ph)
                    s_exp = sem(f"u_expanded_{name}", ph)
                    s_prod = sem(f"products_{name}", ph)
                    s_dot = sem(f"dots_{name}", ph)
                    s_e = sem(f"exponentials_{name}", ph)
                    s_p = sem(f"shares_{name}", ph)
                    s_msg = sem(f"messages_{name}", ph)
                    s_sum = sem(f"summed_{name}", ph)
                    s_acc = sem(f"added_{name}", ph)
                    s_l = sem(f"arithmetic_{name}", ph)
                    s_f = sem(f"sums_and_square_sums_{name}", ph)
                    s_t = sem(f"squares_and_roots_{name}", ph)
                    s_go = sem(f"round_ready_{name}", ph)
                    z_rows = z_tab
                    per = NQ // RING * 16

                    def rounds_of(eng, body):
                        if rounds == 1:
                            body(0)
                        else:
                            with eng.Fori(0, rounds) as r:
                                body(r)

                    def z_in(r, q, s):
                        return gathered(q, s) if gathers else r * per + loaded(q, s)

                    with nc.Block() as block:
                        @block.sync
                        def _(sp):
                            def body(r):
                                def targets(q, s):
                                    load_targets(sp, q, s, dl_b, s_dl, s_oht, base=r * NQ)

                                def source(q, s):
                                    if not isinstance(q, int) or q >= RING:
                                        sp.wait_ge(s_msg, r * NQ + (q - (RING - 1)))
                                    sp.dma_start(z[:, s, :], z_rows[bass.ds(q, 1), :, :]
                                                 .rearrange("q p w -> (q p) w")).then_inc(s_z[s], 16)

                                def keep(q, s):
                                    sp.wait_ge(s_z[s], gathered(q, s))
                                    sp.dma_start(z_rows[bass.ds(q, 1), :, :].rearrange("q p w -> (q p) w"),
                                                 z[:, s, :]).then_inc(s_zst[s], 16)
                                if rounds > 1:
                                    sp.wait_ge(s_go, r)
                                sweep(sp, [(3, targets), (0, keep)] if gathers else [(0, source), (0, targets)])
                            rounds_of(sp, body)
                            if gathers:
                                for s in range(RING):
                                    sp.wait_ge(s_zst[s], per)

                        @block.gpsimd
                        def _(pool):
                            if gathers:
                                def gather(q, s):
                                    pool.wait_ge(s_stage, q + 1)
                                    if not isinstance(q, int) or q >= RING:
                                        pool.wait_ge(s_msg, q - (RING - 1))
                                        pool.sem_inc(s_tick, 1)
                                        pool.wait_ge(s_zst[s], loaded(q, s) - 16)
                                    pool.sem_inc(s_tick, 1)
                                    for c in range(CQ):
                                        nc.gpsimd.indirect_dma_start(
                                            out=z[:, s, c * D:(c + 1) * D], out_offset=None, in_=x3_tab,
                                            in_offset=bass.IndirectOffsetOnAxis(ap=st[:, s, c:c + 1], axis=0))\
                                          .then_inc(s_z[s], 16)
                                sweep(pool, [(0, gather)])
                            else:
                                def body(r):
                                    def message(q, s):
                                        pool.wait_ge(s_p, r * (3 * NQ) + (3 * q + 3))
                                        if not isinstance(q, int) or q >= RING:
                                            pool.wait_ge(s_sum, r * NQ + (q - (RING - 1)))
                                        nc.gpsimd.tensor_tensor(
                                            msg[:, s, :].rearrange("p (k c) -> p k c", c=CD),
                                            z[:, s, :].rearrange("p (k c) -> p k c", c=CD),
                                            ex[:, s, :].unsqueeze(2).broadcast_to([P, CQ * CAPS, CD]),
                                            ALU.mult).then_inc(s_msg, 1)
                                    sweep(pool, [(0, message)])
                                rounds_of(pool, body)

                        @block.vector
                        def _(dve):
                            v = nc.vector
                            LINKS = 1 + 4 + 5

                            def body(r):
                                def stage(q, s):
                                    if not isinstance(q, int) or q >= RING:
                                        dve.wait_ge(s_z[s], gathered(q, s) - 16 * CQ)
                                    v.tensor_copy(st[:, s, :], src_row[:, bass.ds(q * CQ, CQ)]).then_inc(s_stage, 1)

                                def hot(q, s):
                                    dve.wait_ge(s_dl[s], r * per + loaded(q, s))
                                    if not isinstance(q, int) or q >= RING:
                                        dve.wait_ge(s_exp, r * NQ + (q - (RING - 1)))
                                        dve.wait_ge(s_sum, r * NQ + (q - (RING - 1)))
                                    v.tensor_scalar(ohts[:, s].rearrange("p c e -> p (c e)"), dl_b[:, s, :],
                                                    part[:, 0:1], None, ALU.is_equal).then_inc(s_oht, 1)
                                    hot_quad(q, hots[:, s]).then_inc(s_hot, 1)

                                def product(q, s):
                                    dve.wait_ge(s_z[s], z_in(r, q, s))
                                    dve.wait_ge(s_exp, r * NQ + (q + 1))
                                    if not isinstance(q, int) or q >= 2:
                                        dve.wait_ge(s_dot, r * NQ + (q - 1))
                                    v.tensor_tensor(prod[:, s % 2, :], ps[:, s, :], z[:, s, :], ALU.mult)\
                                     .then_inc(s_prod, 1)

                                def reduce(q, s):
                                    dve.wait_ge(s_prod, r * NQ + (q + 1))
                                    if not isinstance(q, int) or q >= RING:
                                        dve.wait_ge(s_e, r * NQ + (q - (RING - 1)))
                                    v.tensor_reduce(dot[:, s, :], prod[:, s % 2, :].rearrange("p (k c) -> p k c", c=CD),
                                                    AX.X, ALU.add).then_inc(s_dot, 1)

                                def shares(q, s):
                                    dve.wait_ge(s_e, r * NQ + (q + 1))
                                    e = ex[:, s, :].rearrange("p (c k) -> p c k", k=CAPS)
                                    n = r * (3 * NQ) + 3 * q
                                    v.tensor_reduce(tot[:, s, :], e, AX.X, ALU.add).then_inc(s_p, 1)
                                    dve.wait_ge(s_p, n + 1)
                                    v.reciprocal(tot[:, s, :], tot[:, s, :]).then_inc(s_p, 1)
                                    dve.wait_ge(s_p, n + 2)
                                    v.tensor_tensor(e, e, tot[:, s, :].unsqueeze(2).broadcast_to([P, CQ, CAPS]),
                                                    ALU.mult).then_inc(s_p, 1)

                                def message(q, s):
                                    dve.wait_ge(s_p, 3 * q + 3)
                                    if not isinstance(q, int) or q >= RING:
                                        dve.wait_ge(s_sum, q - (RING - 1))
                                    v.tensor_tensor(msg[:, s, :].rearrange("p (k c) -> p k c", c=CD),
                                                    z[:, s, :].rearrange("p (k c) -> p k c", c=CD),
                                                    ex[:, s, :].unsqueeze(2).broadcast_to([P, CQ * CAPS, CD]),
                                                    ALU.mult).then_inc(s_msg, 1)

                                def add(q, s):
                                    tiles = tiles_of(DVE_ENGINE, q)
                                    dve.wait_ge(s_sum, r * NQ + (q + 1))
                                    for c in range(CQ):
                                        if c or not isinstance(q, int) or q >= 1:
                                            dve.wait_ge(s_acc, r * (CQ * NQ) + (q * CQ + c))
                                        a = u_sum[:, bass.ds(tiles[c], 1), :].rearrange("p t w -> p (t w)")
                                        v.tensor_tensor(a, ps[:, 4 + s, c * D:(c + 1) * D], a, ALU.add)\
                                         .then_inc(s_acc, 1)
                                round_link = linker(dve, s_l, r * LINKS)
                                round_link(v.tensor_copy(u_sum[:], unit[:]))
                                if gathers:
                                    sweep(dve, [(4, stage), (1, product), (3, hot), (1, reduce), (0, shares),
                                                (0, message), (-1, add)])
                                else:
                                    sweep(dve, [(1, product), (3, hot), (1, reduce), (0, shares), (-2, add)])
                                dve.wait_ge(s_acc, (r + 1) * (CQ * NQ))
                                v.nop().then_inc(s_f, 1)
                                capsule_norm(dve, round_link, u_sum, u_sum, s_f, s_t, r * 2)
                                split_bf16(round_link, u_sum[:], lambda k: u_split[:, :, k, :], u_sq[:])
                                v.nop().then_inc(s_go, 1)
                            rounds_of(dve, body)

                        @block.scalar
                        def _(act):
                            def body(r):
                                def exponential(q, s):
                                    act.wait_ge(s_dot, r * NQ + (q + 1))
                                    if not isinstance(q, int) or q >= RING:
                                        act.wait_ge(s_msg, r * NQ + (q - (RING - 1)))
                                    nc.scalar.activation(ex[:, s, :], dot[:, s, :], ACT.Exp).then_inc(s_e, 1)
                                sweep(act, [(0, exponential)])
                                act.wait_ge(s_f, 2 * r + 1)
                                nc.scalar.activation(u_sq[:], u_sum[:], ACT.Square).then_inc(s_t, 1)
                                act.wait_ge(s_f, 2 * r + 2)
                                nc.scalar.activation(nrm[:], nrm[:], ACT.Sqrt).then_inc(s_t, 1)
                            rounds_of(act, body)

                        @block.tensor
                        def _(pe):
                            def body(r):
                                def expand(q, s):
                                    tiles = tiles_of(PE_ENGINE, q)
                                    pe.wait_ge(s_oht, r * NQ + (q + 1))
                                    if not isinstance(q, int) or q >= RING:
                                        pe.wait_ge(s_prod, r * NQ + (q - (RING - 1)))
                                    for c in range(CQ):
                                        for k in range(3):
                                            last = nc.tensor.matmul(
                                                ps[:, s, c * D:(c + 1) * D], ohts[:, s, c, :],
                                                u_split[:, bass.ds(tiles[c], 1), k, :].rearrange("p t w -> p (t w)"),
                                                start=k == 0, stop=k == 2)
                                    last.then_inc(s_exp, 1)

                                def total(q, s):
                                    pe.wait_ge(s_msg, r * NQ + (q + 1))
                                    pe.wait_ge(s_hot, r * NQ + (q + 1))
                                    if not isinstance(q, int) or q >= RING:
                                        pe.wait_ge(s_acc, r * (CQ * NQ) + (q - (RING - 1)) * CQ)
                                    for c in range(CQ):
                                        last = nc.tensor.matmul(ps[:, 4 + s, c * D:(c + 1) * D], hots[:, s, c, :],
                                                                msg[:, s, c * D:(c + 1) * D], start=True, stop=True)
                                    last.then_inc(s_sum, 1)
                                if rounds > 1:
                                    pe.wait_ge(s_go, r)
                                    pe.sem_inc(s_tick, 1)
                                sweep(pe, [(2, expand), (0, total)])
                            rounds_of(pe, body)

            route("r1", 1, True)
            route("r2", ROUTINGS - 1, False)

            with Phase() as ph:
                ln_dve, ln_act = normalizer("ln3", ph)
                s_l = sem("arithmetic_ln3", ph)
                s_x = sem("result_ready", ph)
                s_o = sem("result_stored", ph)
                with nc.Block() as block:
                    @block.vector
                    def _(dve):
                        link = linker(dve, s_l)
                        link(nc.vector.tensor_tensor(x_sb[:], x_sb[:], u_sum[:], ALU.add))
                        ln_dve(dve, link)
                        nc.vector.nop().then_inc(s_x, 1)

                    @block.scalar
                    def _(act):
                        ln_act(act)

                    @block.sync
                    def _(sp):
                        sp.wait_ge(s_x, 1)
                        sp.dma_start(out[0:(NT - 1) * P, :].rearrange("(t p) d -> p t d", p=P),
                                     x_sb[:, 0:NT - 1, :]).then_inc(s_o, 16)
                        sp.dma_start(out[(NT - 1) * P:N, :], x_sb[0:LAST, NT - 1, :]).then_inc(s_o, 16)
                        sp.wait_ge(s_o, 32)


_INS = ["x", "src", "dst", "edge_type_40", "L0_gnn_rFeatures", "L0_gnn_relation_weights",
        "L0_gnn_loop_weight", "L1_gnn_W", "L1_gnn_att_src", "L1_gnn_att_dst", "L1_gnn_bias",
        "L1_gnn_fc_w", "L1_gnn_fc_b", "L2_gnn_W_proj", "L2_gnn_score_src", "L2_gnn_score_tgt",
        "L2_gnn_W_skip", "L2_gnn_bias"]


def kernel(**inputs):
    import numpy as _np
    import concourse.bacc as _bacc
    from concourse.bass_utils import run_bass_kernel_spmd as _run

    nc = _bacc.Bacc("TRN2", target_bir_lowering=False, num_devices=1)
    arrays, args = {}, []
    for name in _INS:
        a = _np.ascontiguousarray(inputs[name])
        arrays[f"in_{name}"] = a
        args.append(nc.dram_tensor(f"in_{name}", a.shape, mybir.dt.from_np(a.dtype), kind="ExternalInput").ap())
    args.append(nc.dram_tensor("out", [N, D], fp32, kind="ExternalOutput").ap())
    gnn_resnorm_kernel(nc, *args)
    r = _run(nc, [arrays], core_ids=[0])
    return r.results[0]["out"]
```

```python
import concourse.bass as bass
from concourse import mybir
from contextlib import ExitStack

fp32 = mybir.dt.float32
bf16 = mybir.dt.bfloat16
i32 = mybir.dt.int32
ALU = mybir.AluOpType
ACT = mybir.ActivationFunctionType
AX = mybir.AxisListType
DVE_ENGINE = [mybir.EngineType.DVE]
PE_ENGINE = [mybir.EngineType.PE]

P = 128
D = 128
N = 6250
E = 106250
R = 40
HEADS = 4
F1 = 64
F2 = 32
CAPS, CD = 8, 16
ROUTINGS = 6

NT = -(-N // P)
NTP = NT + 1
NP = NTP * P
LAST = N - (NT - 1) * P

EJ = -(-E // P)
ELAST = E - (P - 1) * EJ
SU = 16
EJP = -(-EJ // SU) * SU
RB = 10
EJR = -(-EJ // (2 * RB)) * 2 * RB

NCH = -(-(EJ + NT) // 16) * 16
CQ = 4
NQ = NCH // CQ
RING = 4
SLOTS = P * NCH
OUTSIDE = 1 << 20

SPLIT_W = 3 * HEADS // 2

BIG = 1e30


def sweep(eng, stages, tiles=None):
    def peeled(k):
        if tiles is not None and 0 <= k + tiles.offset < NQ:
            tiles.load(k + tiles.offset, 1)
        for off, fn in stages:
            if 0 <= k + off < NQ:
                fn(k + off, (k + off) % RING)

    first, last = 2, (NQ - 4) // RING
    for k in range(-4, first * RING):
        peeled(k)
    with eng.Fori(first, last) as i:
        if tiles is not None:
            tiles.load(i * RING + tiles.offset, RING)
        for s in range(RING):
            for off, fn in stages:
                fn(i * RING + (s + off), (s + off) % RING)
    for k in range(last * RING, NQ + 4):
        peeled(k)


def first_then_loop(eng, count):
    yield 0
    with eng.Fori(1, count) as i:
        yield i


def gnn_resnorm_kernel(nc, x_in, src_in, dst_in, type_in, rfeat, relw, loopw,
                       w1, att_s, att_d, bias1, fcw, fcb,
                       wproj, sc_s, sc_t, wskip, bias2, out):
    ctx = ExitStack()
    with ctx:
        def sb(name, shape, dt, where=ctx):
            return where.enter_context(nc.sbuf_tensor(name, shape, dt))

        def sem(name, where=None):
            if where is None:
                return ctx.enter_context(nc.semaphore(name))
            where.sems.append(nc.alloc_semaphore(name))
            return where.sems[-1]

        class Phase(ExitStack):

            def __init__(self):
                super().__init__()
                self.sems = []

            def __exit__(self, *exc):
                if self.sems and exc[0] is None:
                    nc.clear_and_free_semaphores(self.sems)
                    nc.all_engine_barrier()
                return super().__exit__(*exc)

        s_tick = sem("waits_taken")
        ps = ctx.enter_context(nc.psum_tensor("ps", [P, 8, 512], fp32))

        y_tab = nc.dram_tensor("y_tab", [NP * R, D], fp32, kind="Internal").ap()
        t1_tab = nc.dram_tensor("t1_tab", [NP, HEADS * F1 + HEADS + SPLIT_W], fp32, kind="Internal").ap()
        t2_tab = nc.dram_tensor("t2_tab", [NP, HEADS * F2 + HEADS + SPLIT_W], fp32, kind="Internal").ap()
        k1_tab = nc.dram_tensor("k1_tab", [NQ, P, CQ, HEADS * F1 + HEADS], fp32, kind="Internal").ap()
        k2_tab = nc.dram_tensor("k2_tab", [NQ, P, CQ, HEADS * F2 + HEADS], fp32, kind="Internal").ap()
        x3_tab = nc.dram_tensor("x3_tab", [NP, D], fp32, kind="Internal").ap()
        z_tab = nc.dram_tensor("z_tab", [NQ, P, CQ * D], fp32, kind="Internal").ap()
        rec_tab = nc.dram_tensor("rec_tab", [SLOTS, 4], i32, kind="Internal").ap()
        dl_tab = nc.dram_tensor("dl_tab", [NCH, P], bf16, kind="Internal").ap()
        oht_tab = nc.dram_tensor("oht_tab", [NQ, P, CQ * P], bf16, kind="Internal").ap()

        x_sb = sb("x_sb", [P, NTP, D], fp32)
        ident = sb("ident", [P, P], fp32)
        ident_b = sb("ident_b", [P, P], bf16)
        lane = sb("lane", [P, P], fp32)
        part = sb("part", [P, 1], fp32)
        y_row = sb("y_row", [P, NCH], i32)
        src_row = sb("src_row", [P, NCH], i32)
        dl_f = sb("dl_f", [P, NCH], fp32)
        chunk_tile = sb("chunk_tile", [1, NCH], i32)

        with Phase() as ph:
            src_e = sb("src_e", [P, EJP], i32, ph)
            dst_e = sb("dst_e", [P, EJP], i32, ph)
            typ_e = sb("typ_e", [P, EJP], i32, ph)
            tile_f = sb("tile_f", [P, EJR], fp32, ph)
            rank = sb("rank", [P, EJR], fp32, ph)
            eid = sb("eid", [P, EJP], fp32, ph)
            tmp_f = sb("tmp_f", [P, EJR], fp32, ph)
            tmp_i = sb("tmp_i", [P, EJR], i32, ph)
            row_i = sb("row_i", [P, EJP], i32, ph)
            pay = sb("pay", [P, EJP, 4], i32, ph)
            blank = sb("blank", [P, NCH, 4], i32, ph)
            tri = sb("tri", [P, P], bf16, ph)
            ones = sb("ones", [P, P], bf16, ph)
            onesf = sb("onesf", [P, P], fp32, ph)
            hot = sb("hot", [P, 2, RB, NT], bf16, ph)
            placed = sb("placed", [P, 2, RB, NT], fp32, ph)
            run = sb("run", [P, NT], fp32, ph)
            nch_f = sb("nch_f", [P, NT], fp32, ph)
            nch_i = sb("nch_i", [P, NT], i32, ph)
            ends = sb("ends", [P, NT], fp32, ph)
            end_col = sb("end_col", [NT, 1], fp32, ph)
            chunk_no = sb("chunk_no", [NT, NCH], fp32, ph)
            past = sb("past", [NT, NCH], fp32, ph)

            s_in = sem("edges_in", ph)
            s_iota = sem("iotas_made", ph)
            s_ms = sem("buffers_cleared", ph)
            s_const = sem("constants_made", ph)
            s_blank = sem("records_blanked", ph)
            s_hot = sem("hot_made", ph)
            s_tot = sem("totals_counted", ph)
            s_pre = sem("prefixes_counted", ph)
            NB = EJR // RB
            s_use = sem("prefixes_used", ph)
            s_v = sem("bucket_arithmetic", ph)
            s_ec = sem("ends_transposed", ph)
            s_past = sem("past_made", ph)
            s_tile = sem("chunk_tiles_summed", ph)

            with nc.Block() as block:
                @block.sync
                def _(sp):
                    sp.wait_ge(s_ms, 1)
                    for a, b in ((src_e, src_in), (dst_e, dst_in), (typ_e, type_in)):
                        sp.dma_start(a[0:P - 1, 0:EJ], b[0:(P - 1) * EJ].rearrange("(p j) -> p j", j=EJ))\
                          .then_inc(s_in, 16)
                        sp.dma_start(a[P - 1:P, 0:ELAST],
                                     b[(P - 1) * EJ:E].rearrange("(p j) -> p j", p=1)).then_inc(s_in, 16)
                    sp.dma_start(x_sb[:, 0:NT - 1, :],
                                 x_in[0:(NT - 1) * P, :].rearrange("(t p) d -> p t d", p=P)).then_inc(s_in, 16)
                    sp.dma_start(x_sb[0:LAST, NT - 1, :], x_in[(NT - 1) * P:N, :]).then_inc(s_in, 16)
                    sp.wait_ge(s_const, 2)
                    sp.dma_start(rec_tab.rearrange("(p c) w -> p c w", p=P), blank[:]).then_inc(s_blank, 16)
                    sp.wait_ge(s_in, 16 * 8)
                    sp.wait_ge(s_blank, 16)

                @block.gpsimd
                def _(pool):
                    nc.gpsimd.iota(lane[:], pattern=[[1, P]], base=0, channel_multiplier=0,
                                   allow_small_or_imprecise_dtypes=True).then_inc(s_iota, 1)
                    nc.gpsimd.iota(part[:], pattern=[[0, 1]], base=0, channel_multiplier=1,
                                   allow_small_or_imprecise_dtypes=True).then_inc(s_iota, 1)
                    nc.gpsimd.iota(eid[:], pattern=[[1, EJP]], base=0, channel_multiplier=EJ,
                                   allow_small_or_imprecise_dtypes=True).then_inc(s_iota, 1)
                    nc.gpsimd.iota(chunk_no[:], pattern=[[1, NCH]], base=0, channel_multiplier=0,
                                   allow_small_or_imprecise_dtypes=True).then_inc(s_iota, 1)

                @block.vector
                def _(dve):
                    v = nc.vector
                    n = [0]

                    def link(ins):
                        n[0] += 1
                        ins.then_inc(s_v, 1)
                        dve.wait_ge(s_v, n[0])

                    for a in (src_e, dst_e, typ_e):
                        link(v.memset(a[:], 0))
                    v.memset(x_sb[:, NT - 1:NTP, :], 0.0).then_inc(s_v, 1)
                    n[0] += 1
                    dve.wait_ge(s_v, n[0])
                    v.memset(tile_f[:], float(NT + 1)).then_inc(s_ms, 1)
                    v.memset(blank[:], 0).then_inc(s_const, 1)
                    dve.wait_ge(s_const, 1)
                    v.memset(blank[:, :, 2:3], -1).then_inc(s_const, 1)
                    link(v.memset(run[:], 0.0))
                    link(v.memset(ones[:], 1.0))
                    link(v.memset(onesf[:], 1.0))
                    link(v.memset(pay[:], 0))
                    dve.wait_ge(s_iota, 4)
                    link(v.tensor_scalar(ident[:], lane[:], part[:, 0:1], None, ALU.is_equal))
                    link(v.tensor_copy(ident_b[:], ident[:]))
                    link(v.tensor_scalar(tri[:], lane[:], part[:, 0:1], None, ALU.is_gt))
                    dve.wait_ge(s_in, 16 * 8)
                    link(v.tensor_single_scalar(tmp_i[:, 0:EJP], dst_e[:], 7, ALU.logical_shift_right))
                    dve.wait_ge(s_ms, 1)
                    link(v.tensor_copy(tile_f[:, 0:EJP], tmp_i[:, 0:EJP]))
                    link(v.tensor_scalar(tmp_f[:, 0:EJP], eid[:], float(E), float(NT + 1), ALU.is_ge, ALU.mult))
                    link(v.tensor_tensor(tile_f[:, 0:EJP], tile_f[:, 0:EJP], tmp_f[:, 0:EJP], ALU.add))
                    link(v.memset(tile_f[:, EJ:EJR], float(NT + 1)))

                    def one_hot(b, s):
                        col = tile_f[:, bass.ds(b * RB, RB)]
                        return v.tensor_tensor(
                            hot[:, s], lane[:, 0:NT].unsqueeze(1).broadcast_to([P, RB, NT]),
                            col.unsqueeze(2).broadcast_to([P, RB, NT]), ALU.is_equal)

                    def count_hot(b, s):
                        if not isinstance(b, int) or b >= 2:
                            dve.wait_ge(s_tot, b - 1)
                        one_hot(b, s).then_inc(s_hot, 1)

                    def pairs(eng, step, after=0):
                        for b in range(2):
                            step(b, b)
                        with eng.Fori(1, NB // 2 - 1) as i:
                            for s in range(2):
                                step(2 * i + s, s)
                        for b in range(NB - 2, NB + after):
                            step(b, b % 2)
                    pairs(dve, count_hot)
                    dve.wait_ge(s_tot, NB)
                    link(v.tensor_copy(run[:], ps[:, 4, 0:NT]))
                    link(v.tensor_scalar(nch_f[:], run[:], float(P - 1), None, ALU.add))
                    link(v.tensor_copy(nch_i[:], nch_f[:]))
                    link(v.tensor_single_scalar(nch_i[:], nch_i[:], 7, ALU.logical_shift_right))
                    link(v.tensor_copy(nch_f[:], nch_i[:]))
                    link(v.tensor_tensor_scan(ends[:], onesf[:, 0:NT], nch_f[:], 0.0, ALU.mult, ALU.add))
                    link(v.tensor_tensor(run[:], ends[:], nch_f[:], ALU.subtract))
                    v.tensor_scalar(run[:], run[:], float(P), None, ALU.mult).then_inc(s_ec, 1)
                    dve.wait_ge(s_ec, 2)
                    link(v.tensor_copy(end_col[:], ps[0:NT, 5, 0:1]))
                    v.tensor_scalar(past[:], chunk_no[:], end_col[:, 0:1], None, ALU.is_ge).then_inc(s_past, 1)

                    def place(b, s):
                        if isinstance(b, int) and b >= NB:
                            pass
                        else:
                            one_hot(b, s).then_inc(s_hot, 1)
                        if isinstance(b, int) and b == 0:
                            return
                        c, t = b - 1, 1 - s
                        dve.wait_ge(s_pre, c + 1)
                        v.tensor_tensor(placed[:, t], ps[:, 2 * t, 0:RB * NT].rearrange("p (j t) -> p j t", t=NT),
                                        run[:].unsqueeze(1).broadcast_to([P, RB, NT]), ALU.add)\
                         .then_inc(s_use, 1)
                        dve.wait_ge(s_use, 3 * c + 1)
                        v.tensor_tensor(run[:], ps[:, 2 * t + 1, 0:NT], run[:], ALU.add).then_inc(s_use, 1)
                        v.tensor_tensor(placed[:, t], placed[:, t], hot[:, t], ALU.mult).then_inc(s_use, 1)
                        dve.wait_ge(s_use, 3 * c + 3)
                        v.tensor_reduce(rank[:, bass.ds(c * RB, RB)], placed[:, t], AX.X, ALU.add)\
                         .then_inc(s_ms, 1)
                    pairs(dve, place, after=1)
                    dve.wait_ge(s_ms, 1 + NB)
                    w = slice(0, EJP)
                    link(v.tensor_copy(row_i[:], rank[:, w]))
                    link(v.tensor_single_scalar(tmp_i[:, w], row_i[:], 7, ALU.logical_shift_right))
                    link(v.tensor_copy(rank[:, w], tmp_i[:, w]))
                    link(v.tensor_single_scalar(tmp_i[:, w], row_i[:], P - 1, ALU.bitwise_and))
                    link(v.tensor_copy(tmp_f[:, w], tmp_i[:, w]))
                    link(v.scalar_tensor_tensor(out=rank[:, w], in0=tmp_f[:, w], scalar=float(NCH),
                                                in1=rank[:, w], op0=ALU.mult, op1=ALU.add))
                    link(v.tensor_scalar(tmp_f[:, w], tile_f[:, w], float(NT), float(OUTSIDE), ALU.is_ge, ALU.mult))
                    link(v.tensor_tensor(rank[:, w], rank[:, w], tmp_f[:, w], ALU.add))
                    link(v.tensor_copy(row_i[:], rank[:, w]))
                    link(v.tensor_copy(rank[:, w], src_e[:]))
                    link(v.tensor_copy(tmp_f[:, w], typ_e[:]))
                    link(v.scalar_tensor_tensor(out=tmp_f[:, w], in0=rank[:, w], scalar=float(R),
                                                in1=tmp_f[:, w], op0=ALU.mult, op1=ALU.add))
                    link(v.tensor_copy(pay[:, :, 0], tmp_f[:, w]))
                    link(v.tensor_copy(pay[:, :, 1], src_e[:]))
                    link(v.tensor_single_scalar(pay[:, :, 2], dst_e[:], P - 1, ALU.bitwise_and))
                    for c in range(2):
                        h = slice(c * NCH // 2, (c + 1) * NCH // 2)
                        dve.wait_ge(s_tile, c + 1)
                        link(v.tensor_copy(chunk_tile[0:1, h], ps[0:1, 6 + c, 0:NCH // 2]))

                @block.tensor
                def _(pe):
                    def count(b, s):
                        pe.wait_ge(s_hot, b + 1)
                        for j in range(RB):
                            last = nc.tensor.matmul(ps[:, 4, 0:NT], ones[:], hot[:, s, j, :],
                                                    start=isinstance(b, int) and b + j == 0,
                                                    stop=isinstance(b, int) and b == NB - 1 and j == RB - 1)
                        last.then_inc(s_tot, 1)

                    def prefix(b, s):
                        pe.wait_ge(s_hot, NB + b + 1)
                        if not isinstance(b, int) or b >= 2:
                            pe.wait_ge(s_ms, 1 + b - 1)
                        pre = ps[:, 2 * s, 0:RB * NT].rearrange("p (j t) -> p j t", t=NT)
                        nc.tensor.matmul(pre, tri[:], hot[:, s], start=True, stop=False)
                        for d in range(1, RB):
                            nc.tensor.matmul(pre[:, d:RB, :], ones[:], hot[:, s, 0:RB - d, :],
                                             start=False, stop=d == RB - 1)
                        for j in range(RB):
                            last = nc.tensor.matmul(ps[:, 2 * s + 1, 0:NT], ones[:], hot[:, s, j, :],
                                                    start=j == 0, stop=j == RB - 1)
                        last.then_inc(s_pre, 1)

                    for step in (count, prefix):
                        for b in range(2):
                            step(b, b)
                        with pe.Fori(1, NB // 2 - 1) as i:
                            for s in range(2):
                                step(2 * i + s, s)
                        for b in range(NB - 2, NB):
                            step(b, b % 2)
                        if step is count:
                            pe.wait_ge(s_ec, 1)
                            nc.tensor.matmul(ps[0:NT, 5, 0:1], ends[0:1, :], onesf[0:1, 0:1], start=True, stop=True)\
                              .then_inc(s_ec, 1)
                    pe.wait_ge(s_past, 1)
                    for c in range(2):
                        nc.tensor.matmul(ps[0:1, 6 + c, 0:NCH // 2], onesf[0:NT, 0:1],
                                         past[:, c * NCH // 2:(c + 1) * NCH // 2], start=True, stop=True)\
                          .then_inc(s_tile, 1)

            w0 = sb("w0", [P, R, D], fp32, ph)
            rf_b = sb("rf_b", [P, R * D], fp32, ph)
            y_out = sb("y_out", [P, 2, 2, 512], fp32, ph)
            xs = sb("xs0", [P, D], fp32, ph)
            xt = sb("xt0", [P, D], fp32, ph)
            st_row = sb("st_row", [P, 2, SU], i32, ph)
            st_pay = sb("st_pay", [P, 2, SU, 4], i32, ph)

            s_w = sem("weights0_in", ph)
            s_st = sem("scatter_staged", ph)
            s_sc = [sem("scattered_even", ph), sem("scattered_odd", ph)]
            s_xs = sem("x_tile_staged", ph)
            s_xtp = sem("x_tile_transposed", ph)
            s_xt = sem("x_tile_ready", ph)
            s_y = sem("y_products", ph)
            s_yc = sem("y_added", ph)
            s_yo = [sem("y_stored_even", ph), sem("y_stored_odd", ph)]
            GRP = R * D // 512
            HB = EJP // SU
            y_view = y_tab.rearrange("(t p r) d -> t p (r d)", p=P, r=R)

            with nc.Block() as block:
                @block.sync
                def _(sp):
                    sp.dma_start(w0[:], relw.rearrange("r d f -> d r f")).then_inc(s_w, 16)
                    sp.dma_start(rf_b[:], rfeat.rearrange("r d -> (r d)").unsqueeze(0).broadcast_to([P, R * D]))\
                      .then_inc(s_w, 16)
                    sp.wait_ge(s_w, 32)

                    with sp.Fori(0, NTP // 2) as i:
                        for g in range(GRP):
                            c = g % (GRP // 2)
                            sp.wait_ge(s_yc, i * (2 * GRP) + (2 * g + 2))
                            sp.dma_start(y_view[bass.ds(2 * i + g // (GRP // 2), 1), :, c * 1024:(c + 1) * 1024]
                                         .rearrange("t p w -> (t p) w"),
                                         y_out[:, g % 2].rearrange("p a w -> p (a w)"))\
                              .then_inc(s_yo[g % 2], 16)
                    for s in range(2):
                        sp.wait_ge(s_yo[s], 16 * (NTP * GRP // 4))

                @block.gpsimd
                def _(pool):
                    with pool.Fori(0, HB // 2) as i:
                        for s in range(2):
                            pool.wait_ge(s_st, i * 4 + (2 * s + 2))
                            pool.sem_inc(s_tick, 1)
                            for j in range(SU):
                                nc.gpsimd.indirect_dma_start(
                                    out=rec_tab, out_offset=bass.IndirectOffsetOnAxis(ap=st_row[:, s, j:j + 1], axis=0),
                                    in_=st_pay[:, s, j, :], in_offset=None,
                                    bounds_check=SLOTS - 1, oob_is_err=False).then_inc(s_sc[s], 16)
                    for s in range(2):
                        pool.wait_ge(s_sc[s], 16 * SU * (HB // 2))

                @block.scalar
                def _(act):
                    for t in first_then_loop(act, NTP):
                        nc.scalar.activation(xs[:], x_sb[:, bass.ds(t, 1), :].rearrange("p t d -> p (t d)"),
                                             ACT.Copy).then_inc(s_xs, 1)
                        act.wait_ge(s_xtp, t + 1)
                        if not isinstance(t, int):
                            act.wait_ge(s_y, t * GRP)
                        nc.scalar.activation(xt[:], ps[:, 7, 0:P], ACT.Copy).then_inc(s_xt, 1)

                @block.tensor
                def _(pe):
                    pe.wait_ge(s_w, 32)
                    for i in first_then_loop(pe, NTP // 2):
                        for a in range(2):
                            pe.wait_ge(s_xs, 2 * i + (a + 1))
                            nc.tensor.transpose(ps[:, 7, 0:P], xs[:], ident[:]).then_inc(s_xtp, 1)
                            pe.wait_ge(s_xt, 2 * i + (a + 1))
                            for g in range(GRP):
                                before = a * GRP + g - 3
                                if before > 0 or not isinstance(i, int):
                                    pe.wait_ge(s_yc, i * (2 * GRP) + before)
                                nc.tensor.matmul(ps[:, (a * GRP + g) % 4, :], xt[:], w0[:, 4 * g:4 * g + 4, :],
                                                 start=True, stop=True).then_inc(s_y, 1)

                @block.vector
                def _(dve):
                    v = nc.vector
                    dve.wait_ge(s_w, 32)
                    stage_at = {3: 0, 13: 1}

                    def add(i, g):
                        dve.wait_ge(s_y, i * (2 * GRP) + (g + 1))
                        d = g // 2
                        if g % 2 == 0 and (d >= 2 or not isinstance(i, int)):
                            dve.wait_ge(s_yo[d % 2], i * (16 * GRP // 2) + 16 * (d // 2))
                        v.tensor_tensor(y_out[:, (g // 2) % 2, g % 2, :], ps[:, g % 4, :],
                                        rf_b[:, (g % GRP) * 512:(g % GRP + 1) * 512], ALU.add).then_inc(s_yc, 1)

                    def stage(h, s):
                        v.tensor_copy(st_row[:, s, :], row_i[:, bass.ds(h * SU, SU)]).then_inc(s_st, 1)
                        v.tensor_copy(st_pay[:, s], pay[:, bass.ds(h * SU, SU), :]).then_inc(s_st, 1)

                    stage(0, 0)
                    stage(1, 1)
                    for i in first_then_loop(dve, NTP // 2):
                        for g in range(2 * GRP):
                            add(i, g)
                            if g in stage_at:
                                s = stage_at[g]
                                dve.wait_ge(s_sc[s], (i + 1) * (16 * SU))
                                stage(2 * i + (2 + s), s)

        with Phase() as ph:
            rec = sb("rec", [P, NCH, 4], i32, ph)
            dl_t = sb("dl_t", [P, -(-NCH // P), P], bf16, ph)
            s_r = sem("records_in", ph)
            s_c = sem("records_unpacked", ph)
            s_t = sem("dl_transposed", ph)
            s_d = sem("dl_rows_ready", ph)
            s_o = sem("dl_rows_stored", ph)
            BL = -(-NCH // P)

            with nc.Block() as block:
                @block.sync
                def _(sp):
                    sp.dma_start(rec[:], rec_tab.rearrange("(p c) w -> p c w", p=P)).then_inc(s_r, 16)
                    sp.wait_ge(s_d, BL)
                    for b in range(BL):
                        rows = min(P, NCH - b * P)
                        sp.dma_start(dl_tab[b * P:b * P + rows, :], dl_t[0:rows, b, :]).then_inc(s_o, 16)
                    sp.wait_ge(s_o, 16 * BL)

                @block.vector
                def _(dve):
                    v = nc.vector
                    dve.wait_ge(s_r, 16)
                    v.tensor_copy(dl_f[:], rec[:, :, 2]).then_inc(s_c, 1)
                    v.tensor_copy(y_row[:], rec[:, :, 0]).then_inc(s_c, 1)
                    v.tensor_copy(src_row[:], rec[:, :, 1]).then_inc(s_c, 1)
                    for b in range(BL):
                        rows = min(P, NCH - b * P)
                        dve.wait_ge(s_t, b + 1)
                        v.tensor_copy(dl_t[0:rows, b, :], ps[0:rows, b, 0:P]).then_inc(s_d, 1)
                    dve.wait_ge(s_c, 3)

                @block.tensor
                def _(pe):
                    pe.wait_ge(s_c, 1)
                    for b in range(BL):
                        rows = min(P, NCH - b * P)
                        nc.tensor.transpose(ps[0:rows, b, 0:P], dl_f[:, b * P:b * P + rows], ident[:])\
                          .then_inc(s_t, 1)

        def stage_and_gather(dve, pool, table, rows, ring, st, s_stage, s_gath, s_free, width):
            def stage(q, s):
                if not isinstance(q, int) or q >= RING:
                    dve.wait_ge(s_gath[s], gathered(q, s) - 16 * CQ)
                nc.vector.tensor_copy(st[:, s, :], rows[:, bass.ds(q * CQ, CQ)]).then_inc(s_stage, 1)

            def gather(q, s):
                pool.wait_ge(s_stage, q + 1)
                if not isinstance(q, int) or q >= RING:
                    pool.wait_ge(s_free, q - (RING - 1))
                pool.sem_inc(s_tick, 1)
                for c in range(CQ):
                    nc.gpsimd.indirect_dma_start(
                        out=ring[:, s, c, 0:width], out_offset=None, in_=table,
                        in_offset=bass.IndirectOffsetOnAxis(ap=st[:, s, c:c + 1], axis=0)).then_inc(s_gath[s], 16)
            return stage, gather

        def gathered(q, s):
            if isinstance(q, int):
                return (q // RING + 1) * 16 * CQ
            return (q - s) * (16 * CQ // RING) + 16 * CQ

        def loaded(q, s):
            if isinstance(q, int):
                return (q // RING + 1) * 16
            return (q - s) * (16 // RING) + 16

        class Tiles:

            def __init__(self, engine, offset):
                self.engine, self.offset = engine, offset

            def load(self, q, quads):
                self.quads = quads
                self.regs = nc.values_load_multi_w_load_instructions(
                    chunk_tile[0:1, bass.ds(q * CQ, quads * CQ)], engines=self.engine, min_val=0, max_val=NT,
                    skip_runtime_bounds_check_because="the number of buckets, of NT, that ended before a chunk")[1]

            def __getitem__(self, at):
                s, c = at
                return self.regs[((s - self.offset) % RING) * CQ + c] if self.quads > 1 else self.regs[c]

        def hot_quad(q, out_ap, op=ALU.is_equal):
            return nc.vector.tensor_tensor(
                out_ap, lane[:].unsqueeze(1).broadcast_to([P, CQ, P]),
                dl_f[:, bass.ds(q * CQ, CQ)].unsqueeze(2).broadcast_to([P, CQ, P]), op)

        def project(name, ph, k, weights, width):
            xs = sb(f"xs_{name}", [P, 2, k * P], fp32, ph)
            xt = sb(f"xt_{name}", [P, 2, k * P], fp32, ph)
            s_xs = sem(f"staged_{name}", ph)
            s_tp = sem(f"transposed_{name}", ph)
            s_xt = sem(f"stationary_{name}", ph)
            s_mm = sem(f"product_{name}", ph)
            s_ev = sem(f"product_read_{name}", ph)

            def tiles(eng, body):
                for t in range(2):
                    body(t, t, True)
                with eng.Fori(1, NTP // 2 - 1) as i:
                    for s in range(2):
                        body(2 * i + s, s, False)
                for t in range(NTP - 2, NTP):
                    body(t, t % 2, False)

            def act_part(act, tile):
                def stage(t, s, early):
                    if not early:
                        act.wait_ge(s_tp, t - 1)
                    nc.scalar.activation(xs[:, s], tile(t), ACT.Copy).then_inc(s_xs, 1)
                tiles(act, stage)

            def pe_part(pe):
                def turn(t, s, early):
                    pe.wait_ge(s_xs, t + 1)
                    if not early:
                        pe.wait_ge(s_xt, t - 1)
                    for b in range(k):
                        last = nc.tensor.transpose(ps[:, 4 + s, b * P:(b + 1) * P],
                                                   xs[:, s, b * P:(b + 1) * P], ident[:])
                    last.then_inc(s_tp, 1)

                def product(t, s, early):
                    pe.wait_ge(s_xt, t + 1)
                    if not early:
                        pe.wait_ge(s_ev, t - 1)
                    for b in range(k):
                        last = nc.tensor.matmul(ps[:, s, 0:width], xt[:, s, b * P:(b + 1) * P],
                                                weights[:, b, :], start=b == 0, stop=b == k - 1)
                    last.then_inc(s_mm, 1)

                def step(t, s, early):
                    product(t, s, early)
                    if not isinstance(t, int) or t + 2 < NTP:
                        turn(t + 2, s, False)
                turn(0, 0, True)
                turn(1, 1, True)
                tiles(pe, step)

            def dve_part(dve, read, ready=None):
                def copy(t, s, early):
                    dve.wait_ge(s_tp, t + 1)
                    if not early:
                        dve.wait_ge(s_mm, t - 1)
                    nc.vector.tensor_copy(xt[:, s], ps[:, 4 + s, 0:k * P]).then_inc(s_xt, 1)

                def step(t, s, early):
                    dve.wait_ge(s_mm, t + 1)
                    if ready is not None and not early:
                        ready(t, s)
                    read(t, s).then_inc(s_ev, 1)
                    if not isinstance(t, int) or t + 2 < NTP:
                        copy(t + 2, s, False)
                copy(0, 0, True)
                copy(1, 1, True)
                tiles(dve, step)
                dve.wait_ge(s_ev, NTP)

            return act_part, pe_part, dve_part

        def tile_of(big):
            return lambda t: big[:, bass.ds(t, 1), :].rearrange("p t d -> p (t d)")

        def normalizer(name, ph):
            sq = sb(f"sq_{name}", [P, NTP, D], fp32, ph)
            mean = sb(f"mean_{name}", [P, NTP], fp32, ph)
            var = sb(f"var_{name}", [P, NTP], fp32, ph)
            std = sb(f"std_{name}", [P, NTP], fp32, ph)
            s_cen = sem(f"centred_{name}", ph)
            s_sq = sem(f"squared_{name}", ph)
            s_var = sem(f"variances_{name}", ph)
            s_std = sem(f"deviations_{name}", ph)

            def dve_part(dve, link):
                v = nc.vector
                link(v.tensor_reduce(mean[:], x_sb[:], AX.X, ALU.add))
                link(v.tensor_scalar(mean[:], mean[:], 1.0 / D, None, ALU.mult))
                v.tensor_tensor(x_sb[:], x_sb[:], mean[:].unsqueeze(2).broadcast_to([P, NTP, D]),
                                ALU.subtract).then_inc(s_cen, 1)
                dve.wait_ge(s_sq, 1)
                link(v.tensor_reduce(var[:], sq[:], AX.X, ALU.add))
                v.tensor_scalar(var[:], var[:], 1.0 / D, 1e-5, ALU.mult, ALU.add).then_inc(s_var, 1)
                dve.wait_ge(s_std, 1)
                link(v.reciprocal(std[:], std[:]))
                link(v.tensor_tensor(x_sb[:], x_sb[:], std[:].unsqueeze(2).broadcast_to([P, NTP, D]), ALU.mult))

            def act_part(act):
                act.wait_ge(s_cen, 1)
                nc.scalar.activation(sq[:], x_sb[:], ACT.Square).then_inc(s_sq, 1)
                act.wait_ge(s_var, 1)
                nc.scalar.activation(std[:], var[:], ACT.Sqrt).then_inc(s_std, 1)

            return dve_part, act_part

        def linker(dve, s, base=0):
            count = [0]

            def link(ins):
                count[0] += 1
                ins.then_inc(s, 1)
                dve.wait_ge(s, base + count[0])
            return link

        acc0 = ctx.enter_context(ExitStack())
        acc = sb("acc", [P, NTP, HEADS * F1 + HEADS], fp32, acc0)

        with Phase() as ph:
            W = D + 1
            ring = sb("ring_0", [P, RING, CQ, W], fp32, ph)
            st = sb("st_0", [P, RING, CQ], i32, ph)
            hots = sb("hots_0", [P, RING, CQ, P], fp32, ph)
            ohts = sb("ohts_0", [P, RING, CQ * P], bf16, ph)
            dl_b = sb("dl_b_0", [P, RING, CQ * P], bf16, ph)
            s_ini = sem("acc_cleared_0", ph)
            s_stage = sem("rows_staged_0", ph)
            s_gath = [sem(f"gathered_0_{s}", ph) for s in range(RING)]
            s_hot = sem("hot_0", ph)
            s_sum = sem("summed_0", ph)
            s_acc = sem("added_0", ph)
            s_dl = [sem(f"targets_0_{s}", ph) for s in range(RING)]
            s_oht = sem("hot_transposed_0", ph)
            s_ost = [sem(f"hot_transposed_stored_0_{s}", ph) for s in range(RING)]

            with nc.Block() as block:
                @block.sync
                def _(sp):
                    def targets(q, s):
                        if not isinstance(q, int) or q >= RING:
                            sp.wait_ge(s_oht, q - (RING - 1))
                        sp.dma_start(dl_b[:, s, :], dl_tab.rearrange("(q c) e -> q (c e)", c=CQ)[bass.ds(q, 1), :]
                                     .broadcast_to([P, CQ * P])).then_inc(s_dl[s], 16)

                    def keep(q, s):
                        sp.wait_ge(s_oht, q + 1)
                        sp.dma_start(oht_tab[bass.ds(q, 1), :, :].rearrange("q n e -> (q n) e"), ohts[:, s, :])\
                          .then_inc(s_ost[s], 16)
                    sweep(sp, [(2, targets), (0, keep)])
                    for s in range(RING):
                        sp.wait_ge(s_ost[s], NQ // RING * 16)

                @block.gpsimd
                def _(pool):
                    pool.wait_ge(s_ini, 2)
                    _, gather = stage_and_gather(None, pool, y_tab, y_row, ring, st, s_stage, s_gath, s_sum, D)
                    sweep(pool, [(0, gather)])

                @block.vector
                def _(dve):
                    nc.vector.memset(acc[:], 0.0).then_inc(s_ini, 1)
                    nc.vector.memset(ring[:], 1.0).then_inc(s_ini, 1)
                    dve.wait_ge(s_ini, 2)
                    stage, _ = stage_and_gather(dve, None, y_tab, y_row, ring, st, s_stage, s_gath, s_sum, D)

                    def hot(q, s):
                        if not isinstance(q, int) or q >= RING:
                            dve.wait_ge(s_sum, q - (RING - 1))
                        hot_quad(q, hots[:, s]).then_inc(s_hot, 1)

                    def turned_hot(q, s):
                        dve.wait_ge(s_dl[s], loaded(q, s))
                        if not isinstance(q, int) or q >= RING:
                            dve.wait_ge(s_ost[s], loaded(q, s) - 16)
                        nc.vector.tensor_scalar(ohts[:, s, :], dl_b[:, s, :], part[:, 0:1], None, ALU.is_equal)\
                          .then_inc(s_oht, 1)

                    tiles = Tiles(DVE_ENGINE, 0)

                    def add(q, s):
                        dve.wait_ge(s_sum, q + 1)
                        if not isinstance(q, int) or q >= 1:
                            dve.wait_ge(s_acc, q * CQ)
                        for c in range(CQ):
                            a = acc[:, bass.ds(tiles[s, c], 1), 0:W].rearrange("p t w -> p (t w)")
                            ins = nc.vector.tensor_tensor(a, ps[:, (s % 2) * CQ + c, 0:W], a, ALU.add)
                            ins.then_inc(s_acc, 1)
                            if c < CQ - 1:
                                dve.wait_ge(s_acc, q * CQ + (c + 1))
                    sweep(dve, [(3, stage), (1, hot), (0, add), (0, turned_hot)], tiles)

                @block.tensor
                def _(pe):
                    def total(q, s):
                        pe.wait_ge(s_hot, q + 1)
                        pe.wait_ge(s_gath[s], gathered(q, s))
                        if not isinstance(q, int) or q >= 2:
                            pe.wait_ge(s_acc, (q - 1) * CQ)
                        for c in range(CQ):
                            last = nc.tensor.matmul(ps[:, (s % 2) * CQ + c, 0:W], hots[:, s, c, :], ring[:, s, c, :],
                                                    start=True, stop=True)
                        last.then_inc(s_sum, 1)
                    sweep(pe, [(0, total)])

        with Phase() as ph:
            h0 = sb("h0", [P, NTP, D], fp32, ph)
            wl = sb("wl", [P, 1, D], fp32, ph)
            deg = sb("deg", [P, NTP], fp32, ph)
            s_w = sem("loop_weight_in", ph)
            s_l = sem("arithmetic_0", ph)
            s_deg = sem("degrees_0", ph)
            s_rt = sem("degree_roots_0", ph)
            s_h = sem("h_ready_0", ph)
            act_p, pe_p, dve_p = project("l0", ph, 1, wl, D)
            ln_dve, ln_act = normalizer("l0", ph)

            with nc.Block() as block:
                @block.sync
                def _(sp):
                    sp.dma_start(wl[:, 0, :], loopw).then_inc(s_w, 16)
                    sp.wait_ge(s_w, 16)

                @block.vector
                def _(dve):
                    v = nc.vector
                    link = linker(dve, s_l)
                    v.tensor_scalar(deg[:], acc[:, :, D], 1.0, None, ALU.max).then_inc(s_deg, 1)
                    dve.wait_ge(s_rt, 1)
                    link(v.reciprocal(deg[:], deg[:]))
                    v.tensor_tensor(h0[:], acc[:, :, 0:D], deg[:].unsqueeze(2).broadcast_to([P, NTP, D]),
                                    ALU.mult).then_inc(s_h, 1)
                    dve.wait_ge(s_h, 1)

                    def read(t, s):
                        a = acc[:, bass.ds(t, 1), 0:D].rearrange("p t d -> p (t d)")
                        return v.tensor_tensor(a, ps[:, s, 0:D], tile_of(h0)(t), ALU.add)
                    dve_p(dve, read)
                    link(v.scalar_tensor_tensor(out=x_sb[:], in0=acc[:, :, 0:D], scalar=0.0, in1=x_sb[:],
                                                op0=ALU.max, op1=ALU.add))
                    ln_dve(dve, link)

                @block.scalar
                def _(act):
                    act.wait_ge(s_deg, 1)
                    nc.scalar.activation(deg[:], deg[:], ACT.Sqrt).then_inc(s_rt, 1)
                    act.wait_ge(s_h, 1)
                    act_p(act, tile_of(h0))
                    ln_act(act)

                @block.tensor
                def _(pe):
                    pe.wait_ge(s_w, 16)
                    pe_p(pe)

        def split_bf16(link, exact, parts, rest):
            v = nc.vector
            link(v.tensor_copy(parts(0), exact))
            link(v.tensor_tensor(rest, exact, parts(0), ALU.subtract))
            link(v.tensor_copy(parts(1), rest))
            link(v.tensor_tensor(rest, rest, parts(1), ALU.subtract))
            link(v.tensor_copy(parts(2), rest))

        def attention_tables(name, ph, f, w_in, s_in, d_in, skip_in, t_tab, a_src, a_dst, skip):
            hf = HEADS * f
            wide = hf + 2 * HEADS + (D if skip_in is not None else 0)
            wts = sb(f"wts_{name}", [P, 1, wide], fp32, ph)
            att = sb(f"att_{name}", [P, 2, hf], fp32, ph)
            prod = sb(f"attw_{name}", [P, 2, hf], fp32, ph)
            rows = sb(f"rows_{name}", [P, 2, hf + HEADS], fp32, ph)
            parts = sb(f"parts_{name}", [P, NTP, 3, HEADS], bf16, ph)
            rest = sb(f"parts_rest_{name}", [P, NTP, HEADS], fp32, ph)
            s_w = sem(f"weights_in_{name}", ph)
            s_l = sem(f"arithmetic_{name}", ph)
            s_wt = sem(f"weights_ready_{name}", ph)
            s_rows = sem(f"rows_ready_{name}", ph)
            s_all = sem(f"all_tiles_{name}", ph)
            s_st = [sem(f"rows_stored_even_{name}", ph), sem(f"rows_stored_odd_{name}", ph)]
            s_as = sem(f"scores_stored_{name}", ph)
            act_p, pe_p, dve_p = project(name, ph, 1, wts, wide)
            tab = t_tab.rearrange("(t p) w -> t p w", p=P)

            with nc.Block() as block:
                @block.sync
                def _(sp):
                    sp.dma_start(wts[:, 0, 0:hf], w_in).then_inc(s_w, 16)
                    sp.dma_start(att[:, 0, :], s_in.unsqueeze(0).broadcast_to([P, hf])).then_inc(s_w, 16)
                    sp.dma_start(att[:, 1, :], d_in.unsqueeze(0).broadcast_to([P, hf])).then_inc(s_w, 16)
                    if skip_in is not None:
                        sp.dma_start(wts[:, 0, hf + 2 * HEADS:wide], skip_in).then_inc(s_w, 16)
                    with sp.Fori(0, NTP // 2) as i:
                        for s in range(2):
                            sp.wait_ge(s_rows, 2 * i + (s + 1))
                            sp.dma_start(tab[bass.ds(2 * i + s, 1), :, 0:hf + HEADS].rearrange("t p w -> (t p) w"),
                                         rows[:, s, :]).then_inc(s_st[s], 16)
                    sp.wait_ge(s_all, 1)
                    sp.dma_start(t_tab[:, hf + HEADS:].rearrange("(t p) w -> p t w", p=P),
                                 parts[:].rearrange("p t k h -> p t (k h)").bitcast(fp32)).then_inc(s_as, 16)
                    sp.wait_ge(s_as, 16)
                    for s in range(2):
                        sp.wait_ge(s_st[s], 16 * (NTP // 2))

                @block.vector
                def _(dve):
                    v = nc.vector
                    link = linker(dve, s_l)
                    dve.wait_ge(s_w, 48 if skip_in is None else 64)
                    link(v.tensor_tensor(prod[:], att[:], wts[:, 0:1, 0:hf].broadcast_to([P, 2, hf]), ALU.mult))
                    v.tensor_reduce(wts[:, 0, hf:hf + 2 * HEADS],
                                    prod[:].rearrange("p a (h f) -> p (a h) f", f=f), AX.X, ALU.add)\
                     .then_inc(s_wt, 1)

                    def free(t, s):
                        dve.wait_ge(s_st[s], t // 2 * 16 if isinstance(t, int) else (t - s) * 8)

                    def read(t, s):
                        v.tensor_copy(rows[:, s, :], ps[:, s, 0:hf + HEADS]).then_inc(s_rows, 1)
                        v.tensor_copy(a_src[:, bass.ds(t, 1), :].rearrange("p t h -> p (t h)"),
                                      ps[:, s, hf:hf + HEADS])
                        if skip is not None:
                            v.tensor_copy(skip[:, bass.ds(t, 1), :].rearrange("p t h -> p (t h)"),
                                          ps[:, s, hf + 2 * HEADS:wide])
                        return v.tensor_copy(a_dst[:, bass.ds(t, 1), :].rearrange("p t h -> p (t h)"),
                                             ps[:, s, hf + HEADS:hf + 2 * HEADS])
                    dve_p(dve, read, free)
                    split_bf16(link, a_src[:], lambda k: parts[:, :, k, :], rest[:])
                    v.nop().then_inc(s_all, 1)

                @block.scalar
                def _(act):
                    act_p(act, tile_of(x_sb))

                @block.tensor
                def _(pe):
                    pe.wait_ge(s_wt, 1)
                    pe_p(pe)

        def source_maximum(name, f, t_tab, keep_tab, most):
            W = HEADS * f + HEADS
            RW = W + SPLIT_W
            HP = 3 * HEADS
            with Phase() as ph:
                ring = sb(f"ring_{name}", [P, RING, CQ, RW], fp32, ph)
                st = sb(f"st_{name}", [P, RING, CQ], i32, ph)
                others = sb(f"others_{name}", [P, RING, CQ, P], bf16, ph)
                parts = sb(f"slot_parts_{name}", [P, RING, CQ * HP], bf16, ph)
                lines = sb(f"lines_{name}", [CQ * HP, RING, P], bf16, ph)
                place_no = sb(f"place_no_{name}", [CQ * HP, CQ * HEADS], fp32, ph)
                pick_3 = sb(f"pick_3_{name}", [CQ * HP, 3, CQ * HEADS], fp32, ph)
                pick_1 = sb(f"pick_1_{name}", [CQ * HP, CQ * HEADS], fp32, ph)
                pick = sb(f"pick_{name}", [CQ * HP, CQ * HEADS, P], bf16, ph)
                far = sb(f"far_{name}", [P, HEADS, P], bf16, ph)
                high = sb(f"high_{name}", [P, 2, CQ, HEADS], fp32, ph)
                s_no = sem(f"place_numbers_{name}", ph)
                s_ini = sem(f"constants_{name}", ph)
                s_l = sem(f"arithmetic_{name}", ph)
                s_stage = sem(f"rows_staged_{name}", ph)
                s_gath = [sem(f"gathered_{name}_{s}", ph) for s in range(RING)]
                s_keep = [sem(f"kept_{name}_{s}", ph) for s in range(RING)]
                s_pack = sem(f"packed_{name}", ph)
                s_turn = sem(f"turned_{name}", ph)
                s_line = sem(f"lines_{name}_ready", ph)
                s_oth = sem(f"others_{name}_made", ph)
                s_spread = sem(f"spread_{name}", ph)
                s_red = sem(f"reduced_{name}", ph)
                s_max = sem(f"maxima_{name}", ph)

                def turned(s):
                    return ps[0:CQ * HP, 4 + s % 2, 0:P // 2].bitcast(bf16)

                with nc.Block() as block:
                    @block.sync
                    def _(sp):
                        def keep(q, s):
                            sp.wait_ge(s_gath[s], gathered(q, s))
                            sp.dma_start(keep_tab[bass.ds(q, 1), :, :, :].rearrange("q p c w -> (q p) c w"),
                                         ring[:, s, :, 0:W]).then_inc(s_keep[s], 16)
                        sweep(sp, [(0, keep)])
                        for s in range(RING):
                            sp.wait_ge(s_keep[s], NQ // RING * 16)

                    @block.gpsimd
                    def _(pool):
                        nc.gpsimd.iota(place_no[:], pattern=[[HP, CQ], [1, HEADS]], base=0, channel_multiplier=0,
                                       allow_small_or_imprecise_dtypes=True).then_inc(s_no, 1)

                        def gather(q, s):
                            pool.wait_ge(s_stage, q + 1)
                            if not isinstance(q, int) or q >= RING:
                                pool.wait_ge(s_pack, q - (RING - 1))
                                pool.sem_inc(s_tick, 1)
                                pool.wait_ge(s_keep[s], loaded(q, s) - 16)
                            pool.sem_inc(s_tick, 1)
                            for c in range(CQ):
                                nc.gpsimd.indirect_dma_start(
                                    out=ring[:, s, c, :], out_offset=None, in_=t_tab,
                                    in_offset=bass.IndirectOffsetOnAxis(ap=st[:, s, c:c + 1], axis=0))\
                                  .then_inc(s_gath[s], 16)
                        sweep(pool, [(0, gather)])

                    @block.vector
                    def _(dve):
                        v = nc.vector
                        link = linker(dve, s_l)
                        link(v.memset(most[:], -BIG))
                        dve.wait_ge(s_no, 1)
                        for k in range(3):
                            link(v.tensor_scalar(pick_3[:, k, :], place_no[:], float(k * HEADS),
                                                 part[0:CQ * HP, 0:1], ALU.add, ALU.is_equal))
                        link(v.tensor_tensor(pick_1[:], pick_3[:, 0, :], pick_3[:, 1, :], ALU.add))
                        link(v.tensor_tensor(pick_1[:], pick_1[:], pick_3[:, 2, :], ALU.add))
                        v.tensor_copy(pick[:], pick_1[:].unsqueeze(2).broadcast_to([CQ * HP, CQ * HEADS, P]))\
                         .then_inc(s_ini, 1)
                        v.tensor_scalar(far[:], ident[:].unsqueeze(1).broadcast_to([P, HEADS, P]), -BIG, None,
                                        ALU.mult).then_inc(s_ini, 1)
                        stage, _ = stage_and_gather(dve, None, t_tab, src_row, ring, st, s_stage, s_gath,
                                                    s_turn, RW)

                        def other(q, s):
                            if not isinstance(q, int) or q >= RING:
                                dve.wait_ge(s_spread, (q - RING) * CQ + CQ)
                            hot_quad(q, others[:, s], ALU.not_equal).then_inc(s_oth, 1)

                        tiles = Tiles(DVE_ENGINE, 0)

                        def reduce(c):
                            def one(q, s):
                                dve.wait_ge(s_spread, q * CQ + (c + 1))
                                v.tensor_reduce(high[:, s % 2, c, :], ps[:, c, :].rearrange("p (h e) -> p h e", e=P),
                                                AX.X, ALU.max).then_inc(s_red, 1)
                            return one

                        def top(c):
                            def one(q, s):
                                dve.wait_ge(s_red, q * CQ + (c + 1))
                                if c or not isinstance(q, int) or q >= 1:
                                    dve.wait_ge(s_max, q * CQ + c)
                                m = most[:, bass.ds(tiles[s, c], 1), :].rearrange("p t h -> p (t h)")
                                v.tensor_tensor(m, high[:, s % 2, c, :], m, ALU.max).then_inc(s_max, 1)
                            return one
                        sweep(dve, [(3, stage), (0, reduce(0)), (0, reduce(1)), (0, top(0)), (0, reduce(2)),
                                    (0, top(1)), (0, reduce(3)), (0, top(2)), (2, other), (0, top(3))], tiles)

                    @block.scalar
                    def _(act):
                        def pack(q, s):
                            act.wait_ge(s_gath[s], gathered(q, s))
                            if not isinstance(q, int) or q >= RING:
                                act.wait_ge(s_turn, q - (RING - 1))
                            nc.scalar.activation(parts[:, s, :].rearrange("p (c w) -> p c w", w=HP),
                                                 ring[:, s].bitcast(bf16)[:, :, 2 * W:2 * RW], ACT.Copy)\
                              .then_inc(s_pack, 1)

                        def line(q, s):
                            act.wait_ge(s_turn, q + 1)
                            if not isinstance(q, int) or q >= RING:
                                act.wait_ge(s_spread, (q - RING) * CQ + CQ)
                            nc.scalar.activation(lines[:, s, :], turned(s), ACT.Copy).then_inc(s_line, 1)
                        sweep(act, [(2, pack), (1, line)])

                    @block.tensor
                    def _(pe):
                        pe.wait_ge(s_ini, 2)

                        def turn(q, s):
                            pe.wait_ge(s_pack, q + 1)
                            if not isinstance(q, int) or q >= 2:
                                pe.wait_ge(s_line, q - 1)
                            pe.sem_inc(s_tick, 1)
                            nc.tensor.transpose(turned(s), parts[:, s, :], ident_b[:])\
                              .then_inc(s_turn, 1)

                        def spread(q, s):
                            pe.wait_ge(s_line, q + 1)
                            pe.wait_ge(s_oth, q + 1)
                            for c in range(CQ):
                                if not isinstance(q, int) or q >= 1:
                                    pe.wait_ge(s_red, (q - 1) * CQ + (c + 1))
                                for h in range(HEADS):
                                    nc.tensor.matmul(ps[:, c, h * P:(h + 1) * P], pick[:, c * HEADS + h, :],
                                                     lines[:, s, :], start=h == 0, stop=False)
                                nc.tensor.matmul(ps[:, c, :], others[:, s, c, :],
                                                 far[:].rearrange("p h e -> p (h e)"), start=False, stop=True)\
                                  .then_inc(s_spread, 1)
                        sweep(pe, [(1, turn), (0, spread)])

        def target_rows(name, ph, a_src, a_dst, most, everywhere, exp_n, own):
            both = sb(f"both_{name}", [P, NTP, 2 * HEADS], fp32, ph)
            rest = sb(f"rest_{name}", [P, NTP, 2 * HEADS], fp32, ph)
            mine = sb(f"mine_{name}", [P, 1], fp32, ph)
            whole = sb(f"whole_{name}", [P, 1], fp32, ph)
            s_l = sem(f"arithmetic_{name}", ph)
            s_m = sem(f"own_maximum_{name}", ph)
            s_g = sem(f"global_maximum_{name}", ph)

            with nc.Block() as block:
                @block.vector
                def _(dve):
                    v = nc.vector
                    link = linker(dve, s_l)
                    link(v.tensor_copy(both[:, :, 0:HEADS], a_dst[:]))
                    if own is not None:
                        link(v.tensor_tensor(most[:], most[:], a_src[:], ALU.max))
                        link(v.tensor_tensor(own[:], a_src[:], a_dst[:], ALU.add))
                        link(v.scalar_tensor_tensor(out=own[:], in0=own[:], scalar=0.2, in1=own[:],
                                                    op0=ALU.mult, op1=ALU.max))
                    link(v.tensor_tensor(most[:], most[:], a_dst[:], ALU.add))
                    m = both[:, :, HEADS:2 * HEADS]
                    link(v.scalar_tensor_tensor(out=m, in0=most[:], scalar=0.2, in1=most[:],
                                                op0=ALU.mult, op1=ALU.max))
                    if everywhere:
                        v.tensor_reduce(mine[:], m, AX.XY, ALU.max).then_inc(s_m, 1)
                        dve.wait_ge(s_g, 1)
                        link(v.memset(m, 0.0))
                        link(v.tensor_scalar(m, m, whole[:, 0:1], None, ALU.add))
                    if own is not None:
                        v.tensor_tensor(own[:], own[:], m, ALU.subtract).then_inc(s_m, 1)
                    split_bf16(link, both[:], lambda k: exp_n[:, :, k, :], rest[:])

                @block.scalar
                def _(act):
                    if own is not None:
                        act.wait_ge(s_m, 1)
                        nc.scalar.activation(own[:], own[:], ACT.Exp).then_inc(s_g, 1)

                @block.gpsimd
                def _(pool):
                    if everywhere:
                        pool.wait_ge(s_m, 1)
                        nc.gpsimd.partition_all_reduce(whole[:], mine[:], P, bass.bass_isa.ReduceOp.max)\
                          .then_inc(s_g, 1)

        def load_hots(sp, q, s, ohts, s_ohl):
            sp.dma_start(ohts[:, s], oht_tab[bass.ds(q, 1), :, :].rearrange("q n e -> (q n) e")).then_inc(s_ohl[s], 16)

        def attend(name, f, t_tab, keep_tab, exp_n, own):
            hf = HEADS * f
            W = hf + HEADS
            PER = 2 if W <= 256 else 1
            HW = 3 * 2 * HEADS
            DEPTH = PER
            POOL_C = 3 if W > 256 else CQ
            with Phase() as ph:
                ring = sb(f"ring_{name}", [P, RING, CQ, W], fp32, ph)
                msg = sb(f"msg_{name}", [P, RING, CQ, W], fp32, ph)
                hots = sb(f"hots_{name}", [P, RING, CQ, P], fp32, ph)
                ohts = sb(f"ohts_{name}", [P, RING, CQ * P], bf16, ph)
                got = sb(f"sent_{name}", [P, RING, CQ, 2 * HEADS], fp32, ph)
                sc = sb(f"sc_{name}", [P, RING, CQ, HEADS], fp32, ph)
                s_ini = sem(f"acc_begun_{name}", ph)
                s_own = sem(f"own_rows_{name}", ph)
                s_row = [sem(f"rows_{name}_{s}", ph) for s in range(RING)]
                s_ohl = [sem(f"hot_transposed_{name}_{s}", ph) for s in range(RING)]
                s_turn = sem(f"hot_turned_{name}", ph)
                s_hot = sem(f"hot_{name}", ph)
                s_exp = sem(f"expanded_{name}", ph)
                s_s = sem(f"scores_{name}", ph)
                s_e = sem(f"exponentials_{name}", ph)
                s_mp = sem(f"messages_pool_{name}", ph)
                s_mv = sem(f"messages_vector_{name}", ph)
                s_sum = sem(f"summed_{name}", ph)
                s_acc = sem(f"added_{name}", ph)

                def sums(s, c):
                    bank = c if PER == 1 else (s % DEPTH) * CQ // PER + c // PER
                    return ps[:, bank, (c % PER) * W:(c % PER) * W + W]

                def turned(s):
                    return ps[:, 4 + s % 2, 0:CQ * P // 2].bitcast(bf16)

                def messages(engine, s, c0, c1):
                    return engine.tensor_tensor(
                        msg[:, s, c0:c1, 0:hf].rearrange("p c (h f) -> p c h f", f=f),
                        ring[:, s, c0:c1, 0:hf].rearrange("p c (h f) -> p c h f", f=f),
                        msg[:, s, c0:c1, hf:W].unsqueeze(3).broadcast_to([P, c1 - c0, HEADS, f]), ALU.mult)

                with nc.Block() as block:
                    @block.sync
                    def _(sp):
                        if own is not None:
                            sp.dma_start(acc[:, :, 0:W], t_tab[:, 0:W].rearrange("(t p) w -> p t w", p=P))\
                              .then_inc(s_own, 16)

                        def rows(q, s):
                            if not isinstance(q, int) or q >= RING:
                                sp.wait_ge(s_mp, q - (RING - 1))
                                if POOL_C < CQ:
                                    sp.wait_ge(s_mv, q - (RING - 1))
                            sp.dma_start(ring[:, s], keep_tab[bass.ds(q, 1), :, :, :]
                                         .rearrange("q p c w -> (q p) c w")).then_inc(s_row[s], 16)

                        def hots_in(q, s):
                            if not isinstance(q, int) or q >= RING:
                                sp.wait_ge(s_turn, q - (RING - 1))
                            sp.sem_inc(s_tick, 1)
                            load_hots(sp, q, s, ohts, s_ohl)
                        sweep(sp, [(1, hots_in), (0, rows)])

                    @block.gpsimd
                    def _(pool):
                        def message(q, s):
                            pool.wait_ge(s_e, q + 1)
                            if not isinstance(q, int) or q >= RING:
                                pool.wait_ge(s_sum, q - (RING - 1))
                            messages(nc.gpsimd, s, 0, POOL_C).then_inc(s_mp, 1)
                        sweep(pool, [(0, message)])

                    @block.vector
                    def _(dve):
                        v = nc.vector
                        if own is None:
                            v.memset(acc[:], 0.0).then_inc(s_ini, 1)
                            dve.wait_ge(s_ini, 1)
                        else:
                            dve.wait_ge(s_own, 16)
                            a = acc[:, :, 0:hf].rearrange("p t (h f) -> p t h f", f=f)
                            v.tensor_tensor(a, a, own[:].unsqueeze(3).broadcast_to([P, NTP, HEADS, f]), ALU.mult)\
                             .then_inc(s_ini, 1)
                            v.tensor_copy(acc[:, :, hf:W], own[:]).then_inc(s_ini, 1)
                            dve.wait_ge(s_ini, 2)

                        def sent(q, s):
                            dve.wait_ge(s_exp, q + 1)
                            v.tensor_reduce(got[:, s].rearrange("p c w -> p (c w)"),
                                            ps[:, 6 + s % 2, 0:CQ * HW].rearrange("p (c k w) -> p c w k", c=CQ, k=3),
                                            AX.X, ALU.add).then_inc(s_s, 1)

                        def score_sum(q, s):
                            dve.wait_ge(s_row[s], loaded(q, s))
                            dve.wait_ge(s_s, q * 5 + 1)
                            if not isinstance(q, int) or q >= RING:
                                dve.wait_ge(s_e, q - (RING - 1))
                            v.tensor_tensor(sc[:, s], ring[:, s, :, hf:W], got[:, s, :, 0:HEADS], ALU.add)\
                             .then_inc(s_s, 1)

                        def score_leak(q, s):
                            dve.wait_ge(s_s, q * 5 + 2)
                            v.scalar_tensor_tensor(out=sc[:, s], in0=sc[:, s], scalar=0.2, in1=sc[:, s],
                                                   op0=ALU.mult, op1=ALU.max).then_inc(s_s, 1)

                        def score_shift(q, s):
                            dve.wait_ge(s_s, q * 5 + 3)
                            v.tensor_tensor(sc[:, s], sc[:, s], got[:, s, :, HEADS:2 * HEADS], ALU.subtract)\
                             .then_inc(s_s, 1)

                        def score_cap(q, s):
                            dve.wait_ge(s_s, q * 5 + 4)
                            v.tensor_scalar(sc[:, s], sc[:, s], 0.0, None, ALU.min).then_inc(s_s, 1)

                        def message(q, s):
                            dve.wait_ge(s_e, q + 1)
                            if not isinstance(q, int) or q >= RING:
                                dve.wait_ge(s_sum, q - (RING - 1))
                            messages(v, s, POOL_C, CQ).then_inc(s_mv, 1)

                        tiles = Tiles(DVE_ENGINE, -2)

                        def add(c):
                            def one(q, s):
                                if c == 0:
                                    dve.wait_ge(s_sum, q + 1)
                                if c or not isinstance(q, int) or q >= 1:
                                    dve.wait_ge(s_acc, q * CQ + c)
                                a = acc[:, bass.ds(tiles[s, c], 1), 0:W].rearrange("p t w -> p (t w)")
                                v.tensor_tensor(a, sums(s, c), a, ALU.add).then_inc(s_acc, 1)
                            return one
                        own_part = [(0, message)] if POOL_C < CQ else []
                        sweep(dve, [(1, sent), (-2, add(0)), (1, score_sum), (-2, add(1)), (1, score_leak),
                                    (-2, add(2)), (1, score_shift), (-2, add(3)), (1, score_cap)] + own_part, tiles)

                    @block.scalar
                    def _(act):
                        def exponential(q, s):
                            act.wait_ge(s_s, q * 5 + 5)
                            if not isinstance(q, int) or q >= RING:
                                act.wait_ge(s_sum, q - (RING - 1))
                            nc.scalar.activation(msg[:, s, :, hf:W], sc[:, s], ACT.Exp).then_inc(s_e, 1)

                        def hot(q, s):
                            act.wait_ge(s_turn, q + 1)
                            if not isinstance(q, int) or q >= RING:
                                act.wait_ge(s_sum, q - (RING - 1))
                            nc.scalar.activation(hots[:, s].rearrange("p c n -> p (c n)"), turned(s),
                                                 ACT.Copy).then_inc(s_hot, 1)
                        sweep(act, [(1, hot), (1, exponential)])

                    @block.tensor
                    def _(pe):
                        tiles = Tiles(PE_ENGINE, 2)

                        def expand(q, s):
                            pe.wait_ge(s_ohl[s], loaded(q, s))
                            if not isinstance(q, int) or q >= 2:
                                pe.wait_ge(s_s, (q - 2) * 5 + 1)
                            for c in range(CQ):
                                last = nc.tensor.matmul(
                                    ps[:, 6 + s % 2, c * HW:(c + 1) * HW], ohts[:, s, c * P:(c + 1) * P],
                                    exp_n[:, bass.ds(tiles[s, c], 1), :, :].rearrange("p t k w -> p (t k w)"),
                                    start=True, stop=True)
                            if not isinstance(q, int) or q >= 2:
                                pe.wait_ge(s_hot, q - 1)
                            for c in range(CQ):
                                turn = nc.tensor.transpose(turned(s)[:, c * P:(c + 1) * P], ohts[:, s, c * P:(c + 1) * P],
                                                           ident_b[:])
                            turn.then_inc(s_turn, 1)
                            last.then_inc(s_exp, 1)

                        def total(q, s):
                            pe.wait_ge(s_mp, q + 1)
                            if POOL_C < CQ:
                                pe.wait_ge(s_mv, q + 1)
                            pe.wait_ge(s_hot, q + 1)
                            for c in range(CQ):
                                if PER == 1 and (not isinstance(q, int) or q >= 1):
                                    pe.wait_ge(s_acc, (q - 1) * CQ + (c + 1))
                                if PER > 1 and c == 0 and (not isinstance(q, int) or q >= DEPTH):
                                    pe.wait_ge(s_acc, (q - DEPTH) * CQ + CQ)
                                last = nc.tensor.matmul(sums(s, c), hots[:, s, c, :], msg[:, s, c, :],
                                                        start=True, stop=True)
                            last.then_inc(s_sum, 1)
                        sweep(pe, [(2, expand), (-1, total)], tiles)

        with Phase() as l1:
            a_src = sb("a_src1", [P, NTP, HEADS], fp32, l1)
            a_dst = sb("a_dst1", [P, NTP, HEADS], fp32, l1)
            most = sb("most1", [P, NTP, HEADS], fp32, l1)
            own = sb("own1", [P, NTP, HEADS], fp32, l1)
            exp_n = sb("exp_n1", [P, NTP, 3, 2 * HEADS], bf16, l1)
            with Phase() as ph:
                attention_tables("t1", ph, F1, w1, att_s.rearrange("h f -> (h f)"), att_d.rearrange("h f -> (h f)"),
                                 None, t1_tab, a_src, a_dst, None)
            source_maximum("m1", F1, t1_tab, k1_tab, most)
            with Phase() as ph:
                target_rows("n1", ph, a_src, a_dst, most, False, exp_n, own)
            attend("e1", F1, t1_tab, k1_tab, exp_n, own)

        with Phase() as ph:
            HF = HEADS * F1
            g1 = sb("g1", [P, NTP, HF], fp32, ph)
            wf = sb("wf", [P, 2, D], fp32, ph)
            b_b = sb("b1_b", [P, HF], fp32, ph)
            fb_b = sb("fb_b", [P, D], fp32, ph)
            den = sb("den1", [P, NTP, HEADS], fp32, ph)
            s_w = sem("fc_in", ph)
            s_l = sem("arithmetic_f1", ph)
            s_g = sem("g_ready", ph)
            s_b = sem("bias_added_1", ph)
            act_p, pe_p, dve_p = project("f1", ph, 2, wf, D)
            with nc.Block() as block:
                @block.sync
                def _(sp):
                    sp.dma_start(wf[:], fcw.rearrange("(k d) n -> d k n", d=P)).then_inc(s_w, 16)
                    sp.dma_start(b_b[:], bias1.unsqueeze(0).broadcast_to([P, HF])).then_inc(s_w, 16)
                    sp.dma_start(fb_b[:], fcb.unsqueeze(0).broadcast_to([P, D])).then_inc(s_w, 16)
                    sp.wait_ge(s_w, 48)

                @block.vector
                def _(dve):
                    v = nc.vector
                    link = linker(dve, s_l)
                    dve.wait_ge(s_w, 48)
                    link(v.reciprocal(den[:], acc[:, :, HF:HF + HEADS]))
                    link(v.tensor_tensor(g1[:].rearrange("p t (h f) -> p t h f", f=F1),
                                         acc[:, :, 0:HF].rearrange("p t (h f) -> p t h f", f=F1),
                                         den[:].unsqueeze(3).broadcast_to([P, NTP, HEADS, F1]), ALU.mult))
                    link(v.tensor_tensor(g1[:], g1[:], b_b[:].unsqueeze(1).broadcast_to([P, NTP, HF]), ALU.add))
                    v.tensor_scalar(g1[:], g1[:], 0.0, None, ALU.max).then_inc(s_g, 1)
                    v.tensor_tensor(x_sb[:], x_sb[:], fb_b[:].unsqueeze(1).broadcast_to([P, NTP, D]), ALU.add)\
                     .then_inc(s_b, 1)
                    dve.wait_ge(s_b, 1)

                    def read(t, s):
                        return v.tensor_tensor(tile_of(x_sb)(t), ps[:, s, 0:D], tile_of(x_sb)(t), ALU.add)
                    dve_p(dve, read)

                @block.scalar
                def _(act):
                    act.wait_ge(s_g, 1)
                    act_p(act, tile_of(g1))

                @block.tensor
                def _(pe):
                    pe.wait_ge(s_w, 48)
                    pe_p(pe)

        def normalize_block(name):
            with Phase() as ph:
                ln_dve, ln_act = normalizer(name, ph)
                s_l = sem(f"arithmetic_{name}", ph)
                with nc.Block() as block:
                    @block.vector
                    def _(dve):
                        ln_dve(dve, linker(dve, s_l))

                    @block.scalar
                    def _(act):
                        ln_act(act)

        normalize_block("ln1")

        with Phase() as l2:
            a_src = sb("a_src2", [P, NTP, HEADS], fp32, l2)
            a_dst = sb("a_dst2", [P, NTP, HEADS], fp32, l2)
            most = sb("most2", [P, NTP, HEADS], fp32, l2)
            exp_n = sb("exp_n2", [P, NTP, 3, 2 * HEADS], bf16, l2)
            skip = sb("skip2", [P, NTP, D], fp32, l2)
            with Phase() as ph:
                attention_tables("t2", ph, F2, wproj, sc_s.rearrange("a h f -> (a h f)"),
                                 sc_t.rearrange("a h f -> (a h f)"), wskip, t2_tab, a_src, a_dst, skip)
            source_maximum("m2", F2, t2_tab, k2_tab, most)
            with Phase() as ph:
                target_rows("n2", ph, a_src, a_dst, most, True, exp_n, None)
            attend("e2", F2, t2_tab, k2_tab, exp_n, None)

            with Phase() as ph:
                b_b = sb("b2_b", [P, D], fp32, ph)
                low = sb("low2", [P, NTP, D], fp32, ph)
                den = sb("den2", [P, NTP, HEADS], fp32, ph)
                s_w = sem("bias2_in", ph)
                s_l = sem("arithmetic_f2", ph)
                s_low = sem("negatives_2", ph)
                s_ex = sem("exponentials_f2", ph)
                with nc.Block() as block:
                    @block.sync
                    def _(sp):
                        sp.dma_start(b_b[:], bias2.unsqueeze(0).broadcast_to([P, D])).then_inc(s_w, 16)
                        sp.wait_ge(s_w, 16)

                    @block.vector
                    def _(dve):
                        v = nc.vector
                        link = linker(dve, s_l)
                        dve.wait_ge(s_w, 16)
                        link(v.tensor_scalar(den[:], acc[:, :, D:D + HEADS], 1e-16, None, ALU.add))
                        link(v.reciprocal(den[:], den[:]))
                        a = acc[:, :, 0:D]
                        link(v.tensor_tensor(a.rearrange("p t (h f) -> p t h f", f=F2),
                                             a.rearrange("p t (h f) -> p t h f", f=F2),
                                             den[:].unsqueeze(3).broadcast_to([P, NTP, HEADS, F2]), ALU.mult))
                        link(v.tensor_tensor(a, a, skip[:], ALU.add))
                        link(v.tensor_tensor(a, a, b_b[:].unsqueeze(1).broadcast_to([P, NTP, D]), ALU.add))
                        v.tensor_scalar(low[:], a, 0.0, None, ALU.min).then_inc(s_low, 1)
                        link(v.scalar_tensor_tensor(out=x_sb[:], in0=a, scalar=0.0, in1=x_sb[:],
                                                    op0=ALU.max, op1=ALU.add))
                        dve.wait_ge(s_ex, 1)
                        link(v.scalar_tensor_tensor(out=x_sb[:], in0=low[:], scalar=-1.0, in1=x_sb[:],
                                                    op0=ALU.add, op1=ALU.add))

                    @block.scalar
                    def _(act):
                        act.wait_ge(s_low, 1)
                        nc.scalar.activation(low[:], low[:], ACT.Exp).then_inc(s_ex, 1)

        normalize_block("ln2")
        acc0.close()

        with Phase() as l3:
            unit = sb("unit", [P, NTP, D], fp32, l3)
            u_sum = sb("u_sum", [P, NTP, D], fp32, l3)
            u = sb("u", [P, NTP, D], fp32, l3)
            u_sq = sb("u_sq", [P, NTP, D], fp32, l3)
            nrm = sb("nrm", [P, NTP * CAPS], fp32, l3)

            def capsule_norm(dve, link, src, dst, s_from, s_to, base):
                v = nc.vector
                dve.wait_ge(s_to, base + 1)
                link(v.tensor_reduce(nrm[:], u_sq[:].rearrange("p t (k c) -> p (t k) c", c=CD), AX.X, ALU.add))
                nc.vector.nop().then_inc(s_from, 1)
                dve.wait_ge(s_to, base + 2)
                link(v.tensor_scalar(nrm[:], nrm[:], 1e-12, None, ALU.max))
                link(v.reciprocal(nrm[:], nrm[:]))
                link(v.tensor_tensor(dst[:].rearrange("p t (k c) -> p (t k) c", c=CD),
                                     src[:].rearrange("p t (k c) -> p (t k) c", c=CD),
                                     nrm[:].unsqueeze(2).broadcast_to([P, NTP * CAPS, CD]), ALU.mult))

            with Phase() as ph:
                s_l = sem("arithmetic_u0", ph)
                s_f = sem("square_sums_u0", ph)
                s_t = sem("squares_and_roots_u0", ph)
                s_u = sem("unit_ready", ph)
                s_o = sem("unit_stored", ph)
                with nc.Block() as block:
                    @block.vector
                    def _(dve):
                        v = nc.vector
                        link = linker(dve, s_l)
                        capsule_norm(dve, link, x_sb, unit, s_f, s_t, 0)
                        v.nop().then_inc(s_u, 1)

                    @block.scalar
                    def _(act):
                        nc.scalar.activation(u_sq[:], x_sb[:], ACT.Square).then_inc(s_t, 1)
                        act.wait_ge(s_f, 1)
                        nc.scalar.activation(nrm[:], nrm[:], ACT.Sqrt).then_inc(s_t, 1)

                    @block.sync
                    def _(sp):
                        sp.wait_ge(s_u, 1)
                        sp.dma_start(x3_tab.rearrange("(t p) d -> p t d", p=P), unit[:]).then_inc(s_o, 16)
                        sp.wait_ge(s_o, 16)

            def route(name, rounds, gathers):
                with Phase() as ph:
                    z = sb(f"z_{name}", [P, RING, CQ * D], fp32, ph)
                    msg = sb(f"msg_{name}", [P, RING, CQ * D], fp32, ph)
                    prod = sb(f"prod_{name}", [P, 2, CQ * D], fp32, ph)
                    st = sb(f"st_{name}", [P, RING, CQ], i32, ph)
                    hots = sb(f"hots_{name}", [P, RING, CQ, P], fp32, ph)
                    ohts = sb(f"ohts_{name}", [P, RING, CQ * P], bf16, ph)
                    wide = sb(f"wide_{name}", [P, RING, CQ * P], fp32, ph)
                    dot = sb(f"dot_{name}", [P, RING, CQ * CAPS], fp32, ph)
                    ex = sb(f"ex_{name}", [P, RING, CQ * CAPS], fp32, ph)
                    tot = sb(f"tot_{name}", [P, RING, CQ], fp32, ph)
                    s_stage = sem(f"rows_staged_{name}", ph)
                    s_z = [sem(f"sources_{name}_{s}", ph) for s in range(RING)]
                    s_zst = [sem(f"sources_stored_{name}_{s}", ph) for s in range(RING)]
                    s_ohl = [sem(f"hot_transposed_{name}_{s}", ph) for s in range(RING)]
                    s_wide = sem(f"hot_widened_{name}", ph)
                    s_u = sem(f"sums_begun_{name}", ph)
                    s_hot = sem(f"hot_{name}", ph)
                    s_exp = sem(f"u_expanded_{name}", ph)
                    s_prod = sem(f"products_{name}", ph)
                    s_dot = sem(f"dots_{name}", ph)
                    s_e = sem(f"exponentials_{name}", ph)
                    s_p = sem(f"shares_{name}", ph)
                    s_msg = sem(f"messages_{name}", ph)
                    s_sum = sem(f"summed_{name}", ph)
                    s_acc = sem(f"added_{name}", ph)
                    s_l = sem(f"arithmetic_{name}", ph)
                    s_f = sem(f"sums_and_square_sums_{name}", ph)
                    s_t = sem(f"squares_and_roots_{name}", ph)
                    s_go = sem(f"round_ready_{name}", ph)
                    s_turn = sem(f"hot_turned_{name}", ph)
                    u_now = unit if gathers else u
                    def turned(s):
                        return ps[:, 6 + s % 2, 0:CQ * P // 2].bitcast(bf16)
                    per = NQ // RING * 16

                    def rounds_of(eng, body):
                        if rounds == 1:
                            body(0)
                        else:
                            with eng.Fori(0, rounds) as r:
                                body(r)

                    def z_in(r, q, s):
                        return gathered(q, s) if gathers else r * per + loaded(q, s)

                    with nc.Block() as block:
                        @block.sync
                        def _(sp):
                            def body(r):
                                def hots_in(q, s):
                                    if not isinstance(q, int) or q >= RING:
                                        sp.wait_ge(s_turn, r * NQ + (q - (RING - 1)))
                                        sp.wait_ge(s_wide, r * NQ + (q - (RING - 1)))
                                    sp.sem_inc(s_tick, 1)
                                    load_hots(sp, q, s, ohts, s_ohl)

                                def source(q, s):
                                    if not isinstance(q, int) or q >= RING:
                                        sp.wait_ge(s_msg, r * NQ + (q - (RING - 1)))
                                    sp.sem_inc(s_tick, 1)
                                    sp.dma_start(z[:, s, :], z_tab[bass.ds(q, 1), :, :]
                                                 .rearrange("q p w -> (q p) w")).then_inc(s_z[s], 16)

                                def keep(q, s):
                                    sp.wait_ge(s_z[s], gathered(q, s))
                                    sp.sem_inc(s_tick, 1)
                                    sp.dma_start(z_tab[bass.ds(q, 1), :, :].rearrange("q p w -> (q p) w"),
                                                 z[:, s, :]).then_inc(s_zst[s], 16)
                                if rounds > 1:
                                    sp.wait_ge(s_go, r + 1)
                                    sp.sem_inc(s_tick, 1)
                                sweep(sp, [(3, hots_in), (0, keep)] if gathers else [(1, hots_in), (0, source)])
                            rounds_of(sp, body)
                            if gathers:
                                for s in range(RING):
                                    sp.wait_ge(s_zst[s], per)

                        @block.gpsimd
                        def _(pool):
                            if gathers:
                                def gather(q, s):
                                    pool.wait_ge(s_stage, q + 1)
                                    if not isinstance(q, int) or q >= RING:
                                        pool.wait_ge(s_msg, q - (RING - 1))
                                        pool.sem_inc(s_tick, 1)
                                        pool.wait_ge(s_zst[s], loaded(q, s) - 16)
                                    pool.sem_inc(s_tick, 1)
                                    for c in range(CQ):
                                        nc.gpsimd.indirect_dma_start(
                                            out=z[:, s, c * D:(c + 1) * D], out_offset=None, in_=x3_tab,
                                            in_offset=bass.IndirectOffsetOnAxis(ap=st[:, s, c:c + 1], axis=0))\
                                          .then_inc(s_z[s], 16)
                                sweep(pool, [(0, gather)])
                            else:
                                def body(r):
                                    def message(q, s):
                                        pool.wait_ge(s_e, r * NQ + (q + 1))
                                        if not isinstance(q, int) or q >= RING:
                                            pool.wait_ge(s_sum, r * NQ + (q - (RING - 1)))
                                        nc.gpsimd.tensor_tensor(
                                            msg[:, s, :].rearrange("p (k c) -> p k c", c=CD),
                                            z[:, s, :].rearrange("p (k c) -> p k c", c=CD),
                                            ex[:, s, :].unsqueeze(2).broadcast_to([P, CQ * CAPS, CD]),
                                            ALU.mult).then_inc(s_msg, 1)
                                    sweep(pool, [(0, message)])
                                rounds_of(pool, body)

                        @block.vector
                        def _(dve):
                            v = nc.vector
                            LINKS = 4

                            def body(r):
                                def stage(q, s):
                                    if not isinstance(q, int) or q >= RING:
                                        dve.wait_ge(s_z[s], gathered(q, s) - 16 * CQ)
                                    v.tensor_copy(st[:, s, :], src_row[:, bass.ds(q * CQ, CQ)]).then_inc(s_stage, 1)

                                def product(q, s):
                                    dve.wait_ge(s_z[s], z_in(r, q, s))
                                    dve.wait_ge(s_exp, r * NQ + (q + 1))
                                    if not isinstance(q, int) or q >= 2:
                                        dve.wait_ge(s_dot, r * NQ + (q - 1))
                                    v.tensor_tensor(prod[:, s % 2, :], ps[:, s, :], z[:, s, :], ALU.mult)\
                                     .then_inc(s_prod, 1)

                                def reduce(q, s):
                                    dve.wait_ge(s_prod, r * NQ + (q + 1))
                                    if not isinstance(q, int) or q >= RING:
                                        dve.wait_ge(s_e, r * NQ + (q - (RING - 1)))
                                    v.tensor_reduce(dot[:, s, :], prod[:, s % 2, :].rearrange("p (k c) -> p k c", c=CD),
                                                    AX.X, ALU.add).then_inc(s_dot, 1)

                                def share_inverse(q, s):
                                    dve.wait_ge(s_e, r * NQ + (q + 1))
                                    v.reciprocal(tot[:, s, :], tot[:, s, :]).then_inc(s_p, 1)

                                def message(q, s):
                                    dve.wait_ge(s_e, q + 1)
                                    if not isinstance(q, int) or q >= RING:
                                        dve.wait_ge(s_sum, q - (RING - 1))
                                    v.tensor_tensor(msg[:, s, :].rearrange("p (k c) -> p k c", c=CD),
                                                    z[:, s, :].rearrange("p (k c) -> p k c", c=CD),
                                                    ex[:, s, :].unsqueeze(2).broadcast_to([P, CQ * CAPS, CD]),
                                                    ALU.mult).then_inc(s_msg, 1)

                                tiles = Tiles(DVE_ENGINE, -2)

                                def add(c):
                                    def one(q, s):
                                        if c == 0 and isinstance(q, int) and q == 0:
                                            dve.wait_ge(s_u, r + 1)
                                        if c == 0:
                                            dve.wait_ge(s_sum, r * NQ + (q + 1))
                                        if c or not isinstance(q, int) or q >= 1:
                                            dve.wait_ge(s_acc, r * (CQ * NQ) + (q * CQ + c))
                                        a = u_sum[:, bass.ds(tiles[s, c], 1), :].rearrange("p t w -> p (t w)")
                                        v.tensor_tensor(a, ps[:, 4 + s % 2, c * D:(c + 1) * D], a, ALU.add)\
                                         .then_inc(s_acc, 1)
                                    return one
                                round_link = linker(dve, s_l, r * LINKS)
                                late = [(0, message)] if gathers else []
                                early = [(4, stage)] if gathers else []
                                sweep(dve, early + [(-2, add(0)), (1, product), (-2, add(1)), (0, share_inverse),
                                                    (-2, add(2)), (1, reduce), (-2, add(3))] + late, tiles)
                                dve.wait_ge(s_acc, (r + 1) * (CQ * NQ))
                                v.nop().then_inc(s_f, 1)
                                capsule_norm(dve, round_link, u_sum, u, s_f, s_t, r * 2)
                                v.nop().then_inc(s_go, 1)
                            v.nop().then_inc(s_go, 1)
                            rounds_of(dve, body)

                        @block.scalar
                        def _(act):
                            def body(r):
                                if rounds > 1:
                                    act.wait_ge(s_go, r + 1)
                                nc.scalar.activation(u_sum[:], unit[:], ACT.Copy).then_inc(s_u, 1)

                                def widen(q, s):
                                    act.wait_ge(s_ohl[s], r * per + loaded(q, s))
                                    if not isinstance(q, int) or q >= RING:
                                        act.wait_ge(s_exp, r * NQ + (q - (RING - 1)))
                                    nc.scalar.activation(wide[:, s, :], ohts[:, s, :], ACT.Copy).then_inc(s_wide, 1)

                                def exponential(q, s):
                                    act.wait_ge(s_dot, r * NQ + (q + 1))
                                    if not isinstance(q, int) or q >= RING:
                                        act.wait_ge(s_msg, r * NQ + (q - (RING - 1)))
                                    for c in range(CQ):
                                        k = slice(c * CAPS, (c + 1) * CAPS)
                                        last = nc.scalar.activation(ex[:, s, k], dot[:, s, k], ACT.Exp,
                                                                    accum_out=tot[:, s, c:c + 1])
                                    last.then_inc(s_e, 1)

                                def hot(q, s):
                                    act.wait_ge(s_turn, r * NQ + (q + 1))
                                    act.wait_ge(s_p, r * NQ + (q + 1))
                                    if not isinstance(q, int) or q >= RING:
                                        act.wait_ge(s_sum, r * NQ + (q - (RING - 1)))
                                    for c in range(CQ):
                                        last = nc.scalar.activation(hots[:, s, c, :], turned(s)[:, c * P:(c + 1) * P],
                                                                    ACT.Copy, scale=tot[:, s, c:c + 1])
                                    last.then_inc(s_hot, 1)
                                sweep(act, [(0, hot), (1, exponential), (3, widen)])
                                act.wait_ge(s_f, 2 * r + 1)
                                nc.scalar.activation(u_sq[:], u_sum[:], ACT.Square).then_inc(s_t, 1)
                                act.wait_ge(s_f, 2 * r + 2)
                                nc.scalar.activation(nrm[:], nrm[:], ACT.Sqrt).then_inc(s_t, 1)
                            rounds_of(act, body)

                        @block.tensor
                        def _(pe):
                            def body(r):
                                tiles = Tiles(PE_ENGINE, 2)

                                def expand(q, s):
                                    pe.wait_ge(s_wide, r * NQ + (q + 1))
                                    if not isinstance(q, int) or q >= RING:
                                        pe.wait_ge(s_prod, r * NQ + (q - (RING - 1)))
                                    for c in range(CQ):
                                        last = nc.tensor.matmul(
                                            ps[:, s, c * D:(c + 1) * D], wide[:, s, c * P:(c + 1) * P],
                                            u_now[:, bass.ds(tiles[s, c], 1), :].rearrange("p t w -> p (t w)"),
                                            start=True, stop=True)
                                    last.then_inc(s_exp, 1)

                                def turn(q, s):
                                    pe.wait_ge(s_ohl[s], r * per + loaded(q, s))
                                    if not isinstance(q, int) or q >= 2:
                                        pe.wait_ge(s_hot, r * NQ + (q - 1))
                                    for c in range(CQ):
                                        last = nc.tensor.transpose(turned(s)[:, c * P:(c + 1) * P],
                                                                   ohts[:, s, c * P:(c + 1) * P], ident_b[:])
                                    last.then_inc(s_turn, 1)

                                def total(q, s):
                                    pe.wait_ge(s_msg, r * NQ + (q + 1))
                                    pe.wait_ge(s_hot, r * NQ + (q + 1))
                                    if not isinstance(q, int) or q >= 2:
                                        pe.wait_ge(s_acc, r * (CQ * NQ) + (q - 1) * CQ)
                                    for c in range(CQ):
                                        last = nc.tensor.matmul(ps[:, 4 + s % 2, c * D:(c + 1) * D], hots[:, s, c, :],
                                                                msg[:, s, c * D:(c + 1) * D], start=True, stop=True)
                                    last.then_inc(s_sum, 1)
                                if rounds > 1:
                                    pe.wait_ge(s_go, r + 1)
                                    pe.sem_inc(s_tick, 1)
                                sweep(pe, [(-1, total), (1, turn), (2, expand)], tiles)
                            rounds_of(pe, body)

            route("r1", 1, True)
            route("r2", ROUTINGS - 1, False)

            with Phase() as ph:
                ln_dve, ln_act = normalizer("ln3", ph)
                s_l = sem("arithmetic_ln3", ph)
                s_x = sem("result_ready", ph)
                s_o = sem("result_stored", ph)
                with nc.Block() as block:
                    @block.vector
                    def _(dve):
                        link = linker(dve, s_l)
                        link(nc.vector.tensor_tensor(x_sb[:], x_sb[:], u[:], ALU.add))
                        ln_dve(dve, link)
                        nc.vector.nop().then_inc(s_x, 1)

                    @block.scalar
                    def _(act):
                        ln_act(act)

                    @block.sync
                    def _(sp):
                        sp.wait_ge(s_x, 1)
                        sp.dma_start(out[0:(NT - 1) * P, :].rearrange("(t p) d -> p t d", p=P),
                                     x_sb[:, 0:NT - 1, :]).then_inc(s_o, 16)
                        sp.dma_start(out[(NT - 1) * P:N, :], x_sb[0:LAST, NT - 1, :]).then_inc(s_o, 16)
                        sp.wait_ge(s_o, 32)


_INS = ["x", "src", "dst", "edge_type_40", "L0_gnn_rFeatures", "L0_gnn_relation_weights",
        "L0_gnn_loop_weight", "L1_gnn_W", "L1_gnn_att_src", "L1_gnn_att_dst", "L1_gnn_bias",
        "L1_gnn_fc_w", "L1_gnn_fc_b", "L2_gnn_W_proj", "L2_gnn_score_src", "L2_gnn_score_tgt",
        "L2_gnn_W_skip", "L2_gnn_bias"]


def kernel(**inputs):
    import numpy as _np
    import concourse.bacc as _bacc
    from concourse.bass_utils import run_bass_kernel_spmd as _run

    nc = _bacc.Bacc("TRN2", target_bir_lowering=False, num_devices=1)
    arrays, args = {}, []
    for name in _INS:
        a = _np.ascontiguousarray(inputs[name])
        arrays[f"in_{name}"] = a
        args.append(nc.dram_tensor(f"in_{name}", a.shape, mybir.dt.from_np(a.dtype), kind="ExternalInput").ap())
    args.append(nc.dram_tensor("out", [N, D], fp32, kind="ExternalOutput").ap())
    gnn_resnorm_kernel(nc, *args)
    r = _run(nc, [arrays], core_ids=[0])
    return r.results[0]["out"]
```
